# Optimizing a Trainium2 kernel written in Bass

```python
import numpy as np
import jax
import jax.numpy as jnp

def _softmax(x, axis=-1):
    return jax.nn.softmax(x, axis=axis)

def _gelu(x):
    return jax.nn.gelu(x, approximate=True)

def _silu(x):
    return jax.nn.silu(x)

def _sigmoid(x):
    return jax.nn.sigmoid(x)

def _layernorm(x, axis=-1, eps=1e-05):
    m = jnp.mean(x, axis=axis, keepdims=True)
    v = jnp.var(x, axis=axis, keepdims=True)
    return (x - m) / jnp.sqrt(v + eps)

def _scatter_add(tgt, idx, src, axis=0):
    return tgt.at[idx].add(src)

def _segment_sum(src, seg, n):
    return jax.ops.segment_sum(src, seg, n)
kernel_name = 'mk_adj_preln_d1_adj_r2_aa505f'

def setup_inputs(seed: int=0):
    np.random.seed(seed)
    _w = jnp.asarray

    def _rec_inputs():
        import jax
        import jax.numpy as jnp
        _gk = jax.random.key(seed)
        x = -0.000929 + 1 * jax.random.normal(jax.random.fold_in(_gk, 1), (8192, 128), jnp.float32)
        _w = (1.0 + jnp.arange(8192, dtype=jnp.float32)) ** (-0.5)
        _w = _w / _w.mean()
        _pij = jnp.clip(0.000488281 * _w[:, None] * _w[None, :], 0.0, 1.0)
        _a = jax.random.uniform(jax.random.fold_in(_gk, 2), (8192, 8192)) < _pij
        adj = _a.astype(jnp.int32)
        return (x, adj)
    x, adj = _rec_inputs()

    def _L0_gnn_setup():
        import jax, jax.numpy as jnp
        import numpy as np
        N = 4096
        IN = 128
        OUT = 128
        THR = 0.0001
        ALPHA = 0.2
        NEG = -1000000000.0
        key = jax.random.key(seed)
        k1, k2, k3, k4 = jax.random.split(key, 4)
        inp = jax.random.normal(k1, (N, IN), jnp.float32)
        W = jax.random.normal(k2, (IN, OUT), jnp.float32) * (1.414 * np.sqrt(2.0 / (IN + OUT)))
        a = jax.random.normal(k3, (2 * OUT, 1), jnp.float32) * (1.414 * np.sqrt(2.0 / (2 * OUT + 1)))
        adj = jax.random.randint(k4, (N, N), 0, 2, jnp.int32)
        return {'input': inp, 'W': W, 'a': a, 'adj': adj, 'M': N}
    _L0_gnn_all = _L0_gnn_setup()
    _L0_gnn_in = {k: v for k, v in _L0_gnn_all.items() if k in ('W', 'a')}
    del _L0_gnn_all
    return {'x': x, 'adj': adj, 'L0_gnn_W': _L0_gnn_in['W'], 'L0_gnn_a': _L0_gnn_in['a']}

def reference(x, adj, L0_gnn_W, L0_gnn_a):
    import jax
    import jax.numpy as jnp

    def _L0_gnn_ref(input, W, a, adj, M):
        import jax, jax.numpy as jnp
        import numpy as np
        N = 4096
        IN = 128
        OUT = 128
        THR = 0.0001
        ALPHA = 0.2
        NEG = -1000000000.0
        h = input @ W
        a_src = a[:OUT, 0]
        a_dst = a[OUT:, 0]
        e = jax.nn.leaky_relu((h[:M] @ a_src)[:, None] + (h @ a_dst)[None, :], negative_slope=ALPHA)
        valid = (adj[:M] > 0) & (h.sum(axis=1) != 0)[None, :]
        att = jax.nn.softmax(jnp.where(valid, e, NEG), axis=1)
        att = jnp.where(valid, att, 0.0)
        L = valid.sum(axis=1).astype(h.dtype)
        top = att.max(axis=1)
        attention = jnp.where(att >= THR, att, 0.0) * L[:, None]
        attention = jnp.where((top > THR)[:, None], attention, 0.0)
        h_prime = attention @ h
        return jax.nn.elu(h[:M] + h_prime)
    h = jnp.maximum(_layernorm(x, axis=-1), 0.0)
    x = x + _L0_gnn_ref(h, L0_gnn_W, L0_gnn_a, adj, 8192)
    return x

_drawn_inputs = setup_inputs


def setup_inputs(seed=0):
    import zlib

    import numpy as np

    out = dict(_drawn_inputs(seed))
    spreads = {}
    factors = {}
    for name, (base, spread) in spreads.items():
        noise = np.random.default_rng([zlib.crc32(name.encode()), seed]).standard_normal(out[name].shape)
        drawn = base * np.exp(spread * noise) if base else spread * noise
        out[name] = jnp.asarray(drawn.astype(out[name].dtype))
    for name, factor in factors.items():
        out[name] = (out[name] * factor).astype(out[name].dtype)
    return out
```

```python
import concourse.bass as bass
from concourse import mybir
from contextlib import ExitStack

FP32 = mybir.dt.float32
BF16 = mybir.dt.bfloat16
I32 = mybir.dt.int32
ALU = mybir.AluOpType
ACT = mybir.ActivationFunctionType
AX = mybir.AxisListType.X

P = 128
LN_EPS = 1e-5
SLOPE = 0.2
THR = 1e-4
BIG = 1e30
VALID_ABOVE = -1e28


def gat_kernel(nc, x, adj, w, a, out):
    N, D = x.shape
    NT = N // P
    HALF = N // 2
    GT = 2
    NG = NT // GT
    NB = NG // 2
    CELLS = 1024
    PACK = N // CELLS
    BANK = 512
    TAKE = 16
    SLOTS = 32
    ROW = D + 1
    QT = 4
    NQ = NT // QT
    NX = 4
    XT = NT // NX
    DIAG = 8
    EXP_OFF = (127 + 10) * CELLS
    PEN = 1 << 20
    EXP_MASK = 0x7F800000

    table = nc.dram_tensor("table", (N, ROW), FP32, kind="Internal").ap()
    d_line = nc.dram_tensor("d_line", (N // P, P), FP32, kind="Internal").ap()

    x_t = x.rearrange("(t p) d -> p t d", p=P)
    out_t = out.rearrange("(t p) d -> p t d", p=P)
    table_t = table.rearrange("(t p) r -> p t r", p=P)
    adj_t = adj.rearrange("(t p) (h c) -> p t h c", p=P, h=2)

    ctx = ExitStack()
    with ctx:
        def sb(name, shape, dt):
            return ctx.enter_context(nc.sbuf_tensor(name, shape, dt))

        def pb(name, shape, dt=FP32):
            return ctx.enter_context(nc.psum_tensor(name, shape, dt))

        def sem(name):
            return ctx.enter_context(nc.semaphore(name))

        adj_ring = sb("adj_ring", [P, 4, HALF], I32)
        mask_ring = sb("mask_ring", [P, 4, HALF], BF16)
        gbuf = sb("gbuf", [P, 2 * GT * SLOTS * ROW], FP32)
        G = gbuf[:, :].rearrange("p (b i k r) -> p b i k r", b=2, i=GT, k=SLOTS)
        ident = sb("ident", [P, P], FP32)
        pack_w = sb("pack_w", [P, PACK, P], BF16)
        cell_no = sb("cell_no", [2, CELLS], BF16)
        cell_w = sb("cell_w", [2, P], BF16)
        s_all = sb("s_all", [P, NT], FP32)
        flag_all = sb("flag_all", [P, NT], FP32)
        V = sb("V", [P, GT, 2, 2 * TAKE], FP32)
        kint = sb("kint", [P, GT, 2 * TAKE], I32)
        cell = sb("cell", [P, GT, 2 * TAKE], I32)
        hib = sb("hib", [P, GT, 2, 2 * TAKE], I32)
        expo = sb("expo", [P, GT, 2, 2 * TAKE], I32)
        cand = sb("cand", [P, GT, 2, 2 * TAKE], FP32)
        rest = sb("rest", [P, GT, 2 * TAKE], FP32)
        mx = sb("mx", [P, 8, GT], FP32)
        top = sb("top", [P, GT, SLOTS], FP32)
        pen = sb("pen", [P, 2, GT, SLOTS], FP32)
        idx = sb("idx", [P, 2, GT, SLOTS], I32)
        pens = sb("pens", [P, GT], FP32)
        need = sb("need", [GT, 2], I32)
        xm = sb("xm", [P, GT, SLOTS], FP32)
        e = sb("e", [P, GT, SLOTS], FP32)
        em = sb("em", [P, GT, SLOTS], FP32)
        q = sb("q", [P, GT, SLOTS], FP32)
        att = sb("att", [P, GT, SLOTS], FP32)
        keep = sb("keep", [P, GT, SLOTS], FP32)
        valid = sb("valid", [P, GT, SLOTS], FP32)
        wts = sb("wts", [P, GT, SLOTS], FP32)
        r_max = sb("r_max", [P, GT], FP32)
        r_sum = sb("r_sum", [P, GT], FP32)
        r_inv = sb("r_inv", [P, GT], FP32)
        r_deg = sb("r_deg", [P, GT], FP32)
        r_gain = sb("r_gain", [P, GT], FP32)
        diag = sb("diag", [P, DIAG, P], FP32)
        x_in = sb("x_in", [P, 2, GT, D], FP32)
        h_in = sb("h_in", [P, 2, GT, ROW], FP32)
        negy = sb("negy", [P, GT, D], FP32)
        expy = sb("expy", [P, GT, D], FP32)
        elu1 = sb("elu1", [P, GT, D], FP32)
        out_sb = sb("out_sb", [P, 2, GT, D], FP32)

        banks = [pb(f"bank{i}", [P, BANK]) for i in range(8)]
        packed = banks[0:4]
        agg = banks[4:6]
        small = banks[6]

        xs = gbuf[:, 0:NT * D].rearrange("p (t d) -> p t d", d=D)
        ts = gbuf[:, NT * D:NT * D + NT * ROW].rearrange("p (t r) -> p t r", r=ROW)
        w_sb = sb("w_sb", [P, D], FP32)
        a_sb = sb("a_sb", [P, 2], FP32)
        wT = sb("wT", [P, P], FP32)
        wa = sb("wa", [P, 2], FP32)
        negmean = sb("negmean", [P, NT], FP32)
        sums = sb("sums", [P, NT], FP32)
        sq = sb("sq", [P, NT], FP32)
        std = sb("std", [P, NT], FP32)
        rstd = sb("rstd", [P, NT], FP32)
        hsum = sb("hsum", [P, NT], FP32)
        hz = sb("hz", [P, NT], FP32)
        d_raw = sb("d_raw", [P, NT], FP32)
        d_ok = sb("d_ok", [P, NT], FP32)
        dT = sb("dT", [NT, P], FP32)
        eps = sb("eps", [P, 1], FP32)
        relT = sb("relT", [P, 2, QT * P], FP32)
        xT_ps = banks[0:2]
        h_ps = banks[2:4]
        ds_ps = banks[4][:, 0:2 * NT].rearrange("p (t c) -> p t c", c=2)
        misc = banks[5]

        f_adj = adj_ring[:, 0:2, :]
        f_tmp = f_adj.rearrange("p h c -> p (h c)").bitcast(FP32)
        f_adj1 = f_adj.rearrange("p h c -> p (h c)")
        f_e = adj_ring[:, 2:4, :].rearrange("p h c -> p (h c)").bitcast(FP32)
        f_d = mask_ring[:, :, :].rearrange("p r c -> p (r c)").bitcast(FP32)
        f_T = gbuf[:, 0:2 * BANK].rearrange("p (b c) -> p b c", b=2)
        f_h = ts
        f_flag_c = sb("f_flag_c", [NT, 1], FP32)
        f_flag = sb("f_flag", [1, NT], I32)
        f_x = sb("f_x", [P, D], FP32)
        f_out = sb("f_out", [P, D], FP32)

        ident0 = sem("ident0")
        consts = sem("consts")
        w_in = sem("w_in")
        x_loaded = [sem(f"x_loaded{c}") for c in range(NX)]
        vchain = sem("vchain")
        vloop = sem("vloop")
        centered = sem("centered")
        squared = sem("squared")
        var_ready = sem("var_ready")
        std_ready = sem("std_ready")
        rstd_ready = sem("rstd_ready")
        wT_ps_ready = sem("wT_ps_ready")
        wT_ready = sem("wT_ready")
        wa_ps_ready = sem("wa_ps_ready")
        wa_ready = sem("wa_ready")
        xT_ready = sem("xT_ready")
        relT_ready = sem("relT_ready")
        h_ps_ready = sem("h_ps_ready")
        h_ready = sem("h_ready")
        table_row_ready = sem("table_row_ready")
        d_ok_ready = sem("d_ok_ready")
        dT_ps_ready = sem("dT_ps_ready")
        dT_ready = sem("dT_ready")
        table_stored = sem("table_stored")
        d_stored = sem("d_stored")
        gbuf_clear = sem("gbuf_clear")

        adj_in = [sem(f"adj_in{r}") for r in range(4)]
        wait_passed = sem("wait_passed")
        mask_ready = sem("mask_ready")
        packed_ready = sem("packed_ready")
        keys_taken = sem("keys_taken")
        idx_ready = sem("idx_ready")
        pens_ready = sem("pens_ready")
        pensT_ready = sem("pensT_ready")
        need_ready = sem("need_ready")
        gathered = [sem(f"gathered{u}") for u in range(2)]
        em_ready = sem("em_ready")
        q_ready = sem("q_ready")
        wts_ready = sem("wts_ready")
        diag_ready = sem("diag_ready")
        diag_used = sem("diag_used")
        xh_in = [sem(f"xh_in{u}") for u in range(2)]
        agg_ready = sem("agg_ready")
        negy_ready = sem("negy_ready")
        expy_ready = sem("expy_ready")
        out_ready = sem("out_ready")
        out_stored = [sem(f"out_stored{u}") for u in range(2)]

        flagT_ready = sem("flagT_ready")
        flag_col_ready = sem("flag_col_ready")
        flag_row_ready = sem("flag_row_ready")
        flags_ready = sem("flags_ready")
        f_const_in = sem("f_const_in")
        f_in = sem("f_in")
        fchain = sem("fchain")
        f_e_ready = sem("f_e_ready")
        f_q_ready = sem("f_q_ready")
        f_w_ready = sem("f_w_ready")
        f_T_ps_ready = sem("f_T_ps_ready")
        f_T_ready = sem("f_T_ready")
        f_agg_ready = sem("f_agg_ready")
        f_negy_ready = sem("f_negy_ready")
        f_expy_ready = sem("f_expy_ready")
        f_out_ready = sem("f_out_ready")
        f_stored = sem("f_stored")

        GATHER_STEPS = [(4, 6), (6, 7), (7, 8), (8, 9), (9, 10), (10, 12), (12, 16), (16, 24), (24, SLOTS)]
        DIAG_STEPS = [(DIAG, 12), (12, 16), (16, SLOTS)]

        F_CHUNKS = N // BANK
        F_CHAIN = 11

        class Order:

            def __init__(self, eng, s, base=0):
                self.eng, self.s, self.base, self.n = eng, s, base, 0

            def then(self, ins):
                ins.then_inc(self.s, 1)
                self.n += 1

            def settle(self, apart=False):
                self.eng.wait_ge(self.s, self.base + self.n)
                if apart:
                    stand_apart(self.eng)

        vloop_end = []
        def stand_apart(eng):
            eng.sem_inc(wait_passed, 1)

        block = ctx.enter_context(nc.Block())

        def loop_bodies(eng, emit):
            emit(0, True, False)
            with eng.Fori(1, NB) as b:
                emit(b, True, True)
            emit(NB, False, True)

        @block.sync
        def _(sp):
            sp.dma_start(w_sb[:, :], w[:, :]).then_inc(w_in, 16)
            for c in range(2):
                sp.dma_start(a_sb[:, c:c + 1], a[c * D:(c + 1) * D, :]).then_inc(w_in, 16)
            for c in range(NX):
                sp.dma_start(xs[:, c * XT:(c + 1) * XT, :], x_t[:, c * XT:(c + 1) * XT, :]).then_inc(x_loaded[c], 16)
            for r in range(4):
                sp.dma_start(adj_ring[:, r, :], adj_t[:, r // 2, r % 2, :]).then_inc(adj_in[r], 16)
            sp.wait_ge(h_ready, NT)
            sp.wait_ge(d_ok_ready, 2)
            sp.dma_start(table_t, ts).then_inc(table_stored, 16)
            sp.wait_ge(dT_ready, 1)
            sp.dma_start(d_line, dT[:, :]).then_inc(d_stored, 16)
            sp.wait_ge(table_stored, 16)

            def adj_loads(g, last):
                if last:
                    return
                for r in range(4):
                    sp.wait_ge(mask_ready, 4 * g + r + 1)
                    sp.dma_start(adj_ring[:, r, :], adj_t[:, GT * (g + 1) + r // 2, r % 2, :]).then_inc(adj_in[r], 16)

            def body(b, ahead, behind, final):
                for u in range(2):
                    g = 2 * b + u
                    if ahead:
                        adj_loads(g, final and u == 1)
                    if behind:
                        sp.wait_ge(out_ready, g - 2 + 1)
                        sp.dma_start(out_t[:, bass.ds(GT * (g - 2), GT), :], out_sb[:, u, :, :]).then_inc(out_stored[u], 16)
                    if ahead:
                        sp.dma_start(x_in[:, u, :, :], x_t[:, bass.ds(GT * g, GT), :]).then_inc(xh_in[u], 16)
                        sp.dma_start(h_in[:, u, :, :], table_t[:, bass.ds(GT * g, GT), :]).then_inc(xh_in[u], 16)

            body(0, True, False, False)
            with sp.Fori(1, NB - 1) as b:
                body(b, True, True, False)
            body(NB - 1, True, True, True)
            body(NB, False, True, False)
            for u in range(2):
                sp.wait_ge(out_stored[u], 16 * NB)

            sp.wait_ge(flags_ready, 1)
            sp.wait_ge(d_stored, 16)
            sp.dma_start(f_d, d_line.rearrange("(o t) p -> o (t p)", o=1).to_broadcast([P, N])).then_inc(f_const_in, 16)
            sp.dma_start(f_h, table_t).then_inc(f_const_in, 16)
            with sp.Fori(0, NT) as t:
                flag = sp.value_load(f_flag[0:1, bass.ds(t, 1)], min_val=0, max_val=1)
                with sp.If(flag > 0):
                    sp.dma_start(f_adj, adj_t[:, t, :, :]).then_inc(f_in, 16)
                    sp.dma_start(f_x[:, :], x_t[:, t, :]).then_inc(f_in, 16)
                    sp.wait_ge(f_out_ready, 2 * (t + 1))
                    sp.dma_start(out_t[:, t, :], f_out[:, :]).then_inc(f_stored, 16)
                    sp.wait_ge(f_stored, 16 * (t + 1))
                    stand_apart(sp)
                with sp.Else():
                    sp.sem_inc(f_in, 32)
                    sp.sem_inc(f_stored, 16)
            sp.wait_ge(f_stored, 16 * NT)

        @block.gpsimd
        def _(pool):
            pool.memset(ident[:, :], 0.0).then_inc(ident0, 1)
            pool.memset(pack_w[:, :, :], 0.0).then_inc(ident0, 1)
            pool.memset(eps[:, :], LN_EPS).then_inc(consts, 1)
            pool.wait_ge(ident0, 2)
            pool.affine_select(out=ident[:, :], in_=ident[:, :], compare_op=ALU.not_equal, fill=1.0, base=0,
                               pattern=[[-1, P]], channel_multiplier=1).then_inc(consts, 1)
            for k in range(PACK):
                pool.affine_select(out=pack_w[:, k, :], in_=pack_w[:, k, :], compare_op=ALU.not_equal,
                                   fill=float(CELLS << k), base=0, pattern=[[-1, P]],
                                   channel_multiplier=1).then_inc(consts, 1)
            pool.iota(cell_no[0:2, :].rearrange("p (a c) -> p a c", c=256), pattern=[[0, CELLS // 256], [1, 256]],
                      base=0, channel_multiplier=0, allow_small_or_imprecise_dtypes=True).then_inc(ident0, 1)
            pool.memset(cell_w[0:2, :], 1.0).then_inc(ident0, 1)
            pool.wait_ge(ident0, 4)
            pool.iota(cell_no[0:1, :].rearrange("p (a c) -> p a c", c=256), pattern=[[1, CELLS // 256], [0, 256]],
                      base=0, channel_multiplier=0, allow_small_or_imprecise_dtypes=True).then_inc(consts, 1)
            pool.memset(cell_w[0:1, :], 256.0).then_inc(consts, 1)

            pool.wait_ge(table_stored, 16)
            pool.memset(gbuf[:, :], 0.0).then_inc(gbuf_clear, 1)
            pool.wait_ge(gbuf_clear, 1)

            def emit(b, ahead, behind):
                if not ahead:
                    return
                for u in range(2):
                    g = 2 * b + u
                    pool.wait_ge(need_ready, g + 1)
                    pool.wait_ge(idx_ready, g + 1)
                    if behind:
                        pool.wait_ge(agg_ready, g - 1)
                    stand_apart(pool)
                    for i in range(GT):
                        left = pool.value_load(need[i:i + 1, u:u + 1], min_val=0, max_val=SLOTS * PEN)

                        def gather(k):
                            pool.indirect_dma_start(
                                out=G[:, u, i, k, :], out_offset=None, in_=table[:, :],
                                in_offset=bass.IndirectOffsetOnAxis(ap=idx[:, u, i, k:k + 1], axis=0),
                                bounds_check=N - 1, oob_is_err=False).then_inc(gathered[u], 16)

                        for k in range(GATHER_STEPS[0][0]):
                            gather(k)
                        for k0, k1 in GATHER_STEPS:
                            with pool.If(left < (SLOTS - k0) * PEN):
                                for k in range(k0, k1):
                                    gather(k)
                            with pool.Else():
                                pool.inc_swdge_sem([gathered[u]], [16 * (k1 - k0)])

            loop_bodies(pool, emit)

        @block.scalar
        def _(act):
            for c in range(NX):
                act.wait_ge(centered, c + 1)
                nc.scalar.activation(ts[:, c * XT:(c + 1) * XT, 0:D], xs[:, c * XT:(c + 1) * XT, :],
                                     ACT.Square).then_inc(squared, 1)
            act.wait_ge(var_ready, NX)
            act.wait_ge(consts, PACK + 4)
            nc.scalar.activation(std[:, :], sq[:, :], ACT.Sqrt, bias=eps[:, 0:1], scale=1.0 / D).then_inc(std_ready, 1)
            act.wait_ge(rstd_ready, 1)
            for n in range(NQ):
                act.wait_ge(h_ps_ready, n + 1)
                for i in range(QT):
                    t = QT * n + i
                    nc.scalar.activation(ts[:, t, 0:D], h_ps[n % 2][:, i * D:(i + 1) * D], ACT.Copy,
                                         scale=rstd[:, t:t + 1], accum_out=hsum[:, t:t + 1]).then_inc(h_ready, 1)

            def emit(b, ahead, behind):
                if not behind:
                    return
                for u in range(2):
                    g = 2 * b + u - 2
                    act.wait_ge(em_ready, g + 1)
                    nc.scalar.activation(q[:, :, :], em[:, :, :], ACT.Exp).then_inc(q_ready, 1)
                    act.wait_ge(wts_ready, g + 1)
                    stand_apart(act)
                    for i in range(GT):
                        left = act.value_load(need[i:i + 1, u:u + 1], min_val=0, max_val=SLOTS * PEN)
                        base = (GT * g + i) * SLOTS

                        def diagonals(k0, k1):
                            for k in range(k0, k1):
                                if behind == "first" and i == 0 and u == 0 and k < DIAG:
                                    pass
                                else:
                                    act.wait_ge(diag_used, base + k - DIAG + 1)
                                nc.scalar.activation(diag[:, k % DIAG, :], ident[:, :], ACT.Copy,
                                                     scale=wts[:, i, k:k + 1]).then_inc(diag_ready, 1)

                        diagonals(0, DIAG)
                        for k0, k1 in DIAG_STEPS:
                            with act.If(left < (SLOTS - k0) * PEN):
                                diagonals(k0, k1)
                            with act.Else():
                                act.drain().then_inc(diag_ready, k1 - k0)
                    act.wait_ge(agg_ready, g + 1)
                    y = agg[u][:, 0:GT * D].rearrange("p (i d) -> p i d", i=GT)
                    nc.scalar.activation(negy[:, :, :], y, ACT.Relu, scale=-1.0).then_inc(negy_ready, 1)
                    act.wait_ge(negy_ready, g + 1)
                    if behind != "first" or u:
                        act.wait_ge(out_ready, g)
                    nc.scalar.activation(expy[:, :, :], negy[:, :, :], ACT.Exp, scale=-1.0).then_inc(expy_ready, 1)

            emit(1, True, "first")
            with act.Fori(2, NB) as b:
                emit(b, True, True)
            emit(NB, False, True)

            act.wait_ge(flags_ready, 1)
            with act.Fori(0, NT) as t:
                flag = act.value_load(f_flag[0:1, bass.ds(t, 1)], min_val=0, max_val=1)
                with act.If(flag > 0):
                    act.wait_ge(f_e_ready, t + 1)
                    nc.scalar.activation(f_e, f_e, ACT.Exp, bias=r_max[:, 0:1]).then_inc(f_q_ready, 1)
                    for c in range(F_CHUNKS):
                        act.wait_ge(f_T_ps_ready, t * F_CHUNKS + c + 1)
                        nc.scalar.activation(f_T[:, c % 2, :], banks[c % 2][:, :], ACT.Copy).then_inc(f_T_ready, 1)
                    act.wait_ge(f_agg_ready, t + 1)
                    nc.scalar.activation(negy[:, 0, :], agg[0][:, 0:D], ACT.Relu, scale=-1.0).then_inc(f_negy_ready, 1)
                    act.wait_ge(f_negy_ready, t + 1)
                    nc.scalar.activation(expy[:, 0, :], negy[:, 0, :], ACT.Exp, scale=-1.0).then_inc(f_expy_ready, 1)
                    act.wait_ge(f_stored, 16 * (t + 1))
                    stand_apart(act)
                with act.Else():
                    act.sem_inc(f_q_ready, 1)
                    act.sem_inc(f_T_ready, F_CHUNKS)
                    act.sem_inc(f_negy_ready, 1)
                    act.sem_inc(f_expy_ready, 1)

        @block.vector
        def _(dve):
            v = Order(dve, vchain)
            for c in range(NX):
                cs = slice(c * XT, (c + 1) * XT)
                dve.wait_ge(x_loaded[c], 16)
                v.then(nc.vector.tensor_reduce(sums[:, cs], xs[:, cs, :], AX, ALU.add))
                v.settle()
                v.then(nc.vector.tensor_scalar(negmean[:, cs], sums[:, cs], -1.0 / D, None, ALU.mult))
                v.settle()
                nc.vector.tensor_tensor(xs[:, cs, :], xs[:, cs, :],
                                        negmean[:, cs].unsqueeze(2).to_broadcast([P, XT, D]),
                                        ALU.add).then_inc(centered, 1)
                if c == 0:
                    dve.wait_ge(wT_ps_ready, 1)
                    nc.vector.tensor_copy(wT[:, :], misc[:, 0:P]).then_inc(wT_ready, 1)
                if c == 1:
                    dve.wait_ge(wa_ps_ready, 1)
                    nc.vector.tensor_copy(wa[:, :], misc[:, P:P + 2]).then_inc(wa_ready, 1)
                if c > 0:
                    dve.wait_ge(squared, c)
                    nc.vector.tensor_reduce(sq[:, (c - 1) * XT:c * XT], ts[:, (c - 1) * XT:c * XT, 0:D], AX,
                                            ALU.add).then_inc(var_ready, 1)
            dve.wait_ge(squared, NX)
            nc.vector.tensor_reduce(sq[:, (NX - 1) * XT:], ts[:, (NX - 1) * XT:, 0:D], AX, ALU.add).then_inc(var_ready, 1)
            dve.wait_ge(std_ready, 1)
            nc.vector.reciprocal(rstd[:, :], std[:, :]).then_inc(rstd_ready, 1)
            for n in range(NQ):
                dve.wait_ge(xT_ready, n + 1)
                if n >= 2:
                    dve.wait_ge(h_ps_ready, n - 1)
                nc.vector.tensor_scalar(relT[:, n % 2, :], xT_ps[n % 2][:, :], 0.0, None, ALU.max).then_inc(relT_ready, 1)
            dve.wait_ge(h_ps_ready, NQ)
            dve.wait_ge(rstd_ready, 1)
            v.then(nc.vector.tensor_tensor(s_all[:, :], ds_ps[:, :, 0], rstd[:, :], ALU.mult))
            v.then(nc.vector.tensor_tensor(d_raw[:, :], ds_ps[:, :, 1], rstd[:, :], ALU.mult))
            dve.wait_ge(h_ready, NT)
            v.then(nc.vector.tensor_scalar(hz[:, :], hsum[:, :], 0.0, -BIG, ALU.is_equal, ALU.mult))
            v.settle()
            nc.vector.tensor_tensor(d_ok[:, :], d_raw[:, :], hz[:, :], ALU.add).then_inc(d_ok_ready, 1)
            dve.wait_ge(d_ok_ready, 1)
            nc.vector.tensor_copy(ts[:, :, D], d_ok[:, :]).then_inc(d_ok_ready, 1)
            dve.wait_ge(dT_ps_ready, 1)
            nc.vector.tensor_copy(dT[:, :], misc[0:NT, 256:256 + P]).then_inc(dT_ready, 1)

            def make_mask(g, r, behind):
                dve.wait_ge(adj_in[r], 16 * (g + 1))
                if behind:
                    dve.wait_ge(packed_ready, 4 * (g - 1) + r + 1)
                nc.vector.tensor_scalar(mask_ring[:, r, :], adj_ring[:, r, :], 0, None, ALU.is_gt).then_inc(mask_ready, 1)

            def take_keys(g, i, o):
                dve.wait_ge(packed_ready, 4 * g + 2 * i + 2)
                stand_apart(dve)
                for half in range(TAKE // 8):
                    for bk in range(2):
                        c0 = bk * TAKE + 8 * half
                        ins = nc.vector.max(V[:, i, 0, c0:c0 + 8], packed[2 * i + bk][:, :])
                        if half == TAKE // 8 - 1 and bk == 1:
                            ins.then_inc(keys_taken, 1)
                        else:
                            o.then(ins)
                    if half < TAKE // 8 - 1:
                        o.settle(apart=True)
                        for bk in range(2):
                            c0 = bk * TAKE + 8 * half
                            o.then(nc.vector.match_replace(out=packed[2 * i + bk][:, :], in_to_replace=V[:, i, 0, c0:c0 + 8],
                                                           in_values=packed[2 * i + bk][:, :], imm_value=-1.0))
                        o.settle(apart=True)

            def decode(g, u, o):
                o.settle()
                dve.wait_ge(keys_taken, GT * (g + 1))
                o.then(nc.vector.tensor_copy(kint[:, :, :], V[:, :, 0, :]))
                o.then(nc.vector.tensor_scalar(hib[:, :, 0, :], V[:, :, 0, :].bitcast(I32), EXP_MASK, None, ALU.bitwise_and))
                o.settle()
                o.then(nc.vector.tensor_scalar(cell[:, :, :], kint[:, :, :], CELLS - 1, None, ALU.bitwise_and))
                o.then(nc.vector.tensor_tensor(V[:, :, 1, :], V[:, :, 0, :], hib[:, :, 0, :].bitcast(FP32), ALU.subtract))
                o.settle()
                o.then(nc.vector.tensor_scalar(expo[:, :, :, :], V[:, :, :, :].bitcast(I32), 23, None, ALU.logical_shift_right))
                o.then(nc.vector.tensor_scalar(hib[:, :, 1, :], V[:, :, 1, :].bitcast(I32), EXP_MASK, None, ALU.bitwise_and))
                o.settle()
                for level in range(2):
                    o.then(nc.vector.scalar_tensor_tensor(cand[:, :, level, :], expo[:, :, level, :], float(CELLS),
                                                          cell[:, :, :], ALU.mult, ALU.add))
                o.then(nc.vector.tensor_tensor(rest[:, :, :], V[:, :, 1, :], hib[:, :, 1, :].bitcast(FP32), ALU.subtract))
                o.settle(apart=True)
                flat = [cand[:, i, :, :].rearrange("p l k -> p (l k)") for i in range(GT)]
                for k in range(0, SLOTS, 8):
                    for i in range(GT):
                        o.then(nc.vector.max(top[:, i, k:k + 8], flat[i]))
                    if k == 0:
                        o.then(nc.vector.tensor_reduce(mx[:, 0, :], rest[:, :, :], AX, ALU.max))
                    if k == 8:
                        o.then(nc.vector.tensor_tensor(mx[:, 1, :], V[:, :, 0, TAKE - 1], V[:, :, 0, 2 * TAKE - 1], ALU.max))
                    if k == 16:
                        o.then(nc.vector.tensor_tensor(mx[:, 2, :], mx[:, 0, :], mx[:, 1, :], ALU.max))
                    o.settle(apart=True)
                    if k + 8 < SLOTS:
                        for i in range(GT):
                            o.then(nc.vector.match_replace(out=flat[i], in_to_replace=top[:, i, k:k + 8],
                                                           in_values=flat[i], imm_value=0.0))
                        if k == 16:
                            o.then(nc.vector.tensor_scalar(mx[:, 3, :], mx[:, 2, :], float(CELLS), None, ALU.is_ge))
                        o.settle(apart=True)
                o.then(nc.vector.tensor_scalar(pen[:, u, :, :], top[:, :, :], float(EXP_OFF), float(PEN), ALU.is_lt, ALU.mult))
                o.then(nc.vector.scalar_tensor_tensor(flag_all[:, bass.ds(GT * g, GT)], top[:, :, SLOTS - 1], float(EXP_OFF),
                                                      mx[:, 3, :], ALU.is_ge, ALU.max))
                o.settle()
                nc.vector.tensor_reduce(pens[:, :], pen[:, u, :, :], AX, ALU.add).then_inc(pens_ready, 1)
                nc.vector.scalar_tensor_tensor(idx[:, u, :, :], top[:, :, :], float(-EXP_OFF), pen[:, u, :, :],
                                               ALU.add, ALU.add).then_inc(idx_ready, 1)

            def scores(b, g, u, o):
                dve.wait_ge(gathered[u], 16 * GT * SLOTS * b)
                o.then(nc.vector.scalar_tensor_tensor(xm[:, :, :], pen[:, u, :, :], -BIG / PEN, G[:, u, :, :, D],
                                                      ALU.mult, ALU.add))
                o.settle()
                o.then(nc.vector.tensor_tensor(att[:, :, :], xm[:, :, :],
                                               s_all[:, bass.ds(GT * g, GT)].unsqueeze(2).to_broadcast([P, GT, SLOTS]),
                                               ALU.add))
                o.settle()
                o.then(nc.vector.scalar_tensor_tensor(e[:, :, :], att[:, :, :], SLOPE, att[:, :, :], ALU.mult, ALU.max))
                o.settle()
                o.then(nc.vector.tensor_reduce(r_max[:, :], e[:, :, :], AX, ALU.max))
                o.then(nc.vector.tensor_scalar(valid[:, :, :], e[:, :, :], VALID_ABOVE, None, ALU.is_gt))
                o.settle()
                nc.vector.tensor_tensor(em[:, :, :], e[:, :, :], r_max[:, :].unsqueeze(2).to_broadcast([P, GT, SLOTS]),
                                        ALU.subtract).then_inc(em_ready, 1)
                o.then(nc.vector.tensor_reduce(r_deg[:, :], valid[:, :, :], AX, ALU.add))

            def weights(g, u, o, first):
                dve.wait_ge(q_ready, g + 1)
                o.then(nc.vector.tensor_reduce(r_sum[:, :], q[:, :, :], AX, ALU.add))
                o.settle()
                o.then(nc.vector.reciprocal(r_inv[:, :], r_sum[:, :]))
                o.settle()
                o.then(nc.vector.tensor_tensor(att[:, :, :], q[:, :, :],
                                               r_inv[:, :].unsqueeze(2).to_broadcast([P, GT, SLOTS]), ALU.mult))
                o.then(nc.vector.scalar_tensor_tensor(r_gain[:, :], r_inv[:, :], THR, r_deg[:, :], ALU.is_gt, ALU.mult))
                o.settle()
                o.then(nc.vector.scalar_tensor_tensor(keep[:, :, :], att[:, :, :], THR, att[:, :, :], ALU.is_ge, ALU.mult))
                o.settle()
                nc.vector.tensor_tensor(wts[:, :, :], keep[:, :, :],
                                        r_gain[:, :].unsqueeze(2).to_broadcast([P, GT, SLOTS]), ALU.mult).then_inc(wts_ready, 1)

            def finish(b, g, u, o):
                dve.wait_ge(expy_ready, g + 1)
                dve.wait_ge(xh_in[u], 32 * b)
                y = agg[u][:, 0:GT * D].rearrange("p (i d) -> p i d", i=GT)
                o.then(nc.vector.scalar_tensor_tensor(elu1[:, :, :], y, 0.0, expy[:, :, :], ALU.max, ALU.add))
                o.settle()
                if not (isinstance(b, int) and b == 1):
                    dve.wait_ge(out_stored[u], 16 * (b - 1))
                nc.vector.scalar_tensor_tensor(out_sb[:, u, :, :], elu1[:, :, :], -1.0, x_in[:, u, :, :],
                                               ALU.add, ALU.add).then_inc(out_ready, 1)

            def emit(b, ahead, behind, o):
                for u in range(2):
                    g = 2 * b + u
                    more = behind or u
                    if ahead:
                        make_mask(g, 0, more)
                        make_mask(g, 1, more)
                    if behind:
                        scores(b, g - 2, u, o)
                    if ahead:
                        make_mask(g, 2, more)
                    if behind:
                        weights(g - 2, u, o, False)
                    if ahead:
                        make_mask(g, 3, more)
                        take_keys(g, 0, o)
                        take_keys(g, 1, o)
                        decode(g, u, o)
                    if behind:
                        finish(b, g - 2, u, o)
                    if ahead:
                        dve.wait_ge(pensT_ready, g + 1)
                        nc.vector.tensor_reduce(need[:, u:u + 1], small[0:GT, 0:P], AX, ALU.min).then_inc(need_ready, 1)

            o = Order(dve, vloop)
            emit(0, True, False, o)
            first = o.n
            emit(1, True, True, o)
            peeled, per_body = o.n, o.n - first
            with dve.Fori(2, NB) as b:
                o = Order(dve, vloop, peeled + (b - 2) * per_body)
                emit(b, True, True, o)
            assert o.n == per_body
            o = Order(dve, vloop, peeled + (NB - 2) * per_body)
            emit(NB, False, True, o)
            o.settle()
            vloop_end.append(o.base + o.n)

            dve.wait_ge(flagT_ready, 1)
            nc.vector.tensor_reduce(f_flag_c[:, :], small[0:NT, 128:128 + P], AX, ALU.max).then_inc(flag_col_ready, 1)
            dve.wait_ge(flag_row_ready, 1)
            nc.vector.tensor_copy(f_flag[:, :], small[0:1, 256:256 + NT]).then_inc(flags_ready, 1)
            dve.wait_ge(flags_ready, 1)

            dve.wait_ge(f_const_in, 32)
            with dve.Fori(0, NT) as t:
                flag = dve.value_load(f_flag[0:1, bass.ds(t, 1)], min_val=0, max_val=1)
                with dve.If(flag > 0):
                    s_t = s_all[:, bass.ds(t, 1)]
                    o = Order(dve, fchain, t * F_CHAIN)
                    dve.wait_ge(f_in, 32 * (t + 1))
                    o.then(nc.vector.tensor_scalar(f_e, f_adj1, 0, -BIG, ALU.is_le, ALU.mult))
                    o.settle()
                    o.then(nc.vector.tensor_tensor(f_e, f_e, f_d, ALU.add))
                    o.settle()
                    o.then(nc.vector.tensor_scalar(f_e, f_e, s_t, None, ALU.add))
                    o.settle()
                    o.then(nc.vector.scalar_tensor_tensor(f_e, f_e, SLOPE, f_e, ALU.mult, ALU.max))
                    o.settle()
                    o.then(nc.vector.tensor_reduce(r_sum[:, 0:1], f_e, AX, ALU.max))
                    o.then(nc.vector.tensor_scalar(f_tmp, f_e, VALID_ABOVE, None, ALU.is_gt))
                    o.settle()
                    o.then(nc.vector.tensor_reduce(r_deg[:, 0:1], f_tmp, AX, ALU.add))
                    nc.vector.tensor_scalar(r_max[:, 0:1], r_sum[:, 0:1], -1.0, None, ALU.mult).then_inc(f_e_ready, 1)
                    dve.wait_ge(f_q_ready, t + 1)
                    o.settle()
                    o.then(nc.vector.tensor_reduce(r_sum[:, 0:1], f_e, AX, ALU.add))
                    o.settle()
                    o.then(nc.vector.reciprocal(r_inv[:, 0:1], r_sum[:, 0:1]))
                    o.settle()
                    o.then(nc.vector.tensor_scalar(f_tmp, f_e, r_inv[:, 0:1], None, ALU.mult))
                    o.then(nc.vector.scalar_tensor_tensor(r_gain[:, 0:1], r_inv[:, 0:1], THR, r_deg[:, 0:1], ALU.is_gt, ALU.mult))
                    o.settle()
                    nc.vector.scalar_tensor_tensor(f_e, f_tmp, THR, f_tmp, ALU.is_ge, ALU.mult).then_inc(f_w_ready, 1)
                    assert o.n == F_CHAIN, o.n
                    dve.wait_ge(f_w_ready, 2 * t + 1)
                    nc.vector.tensor_scalar(f_e, f_e, r_gain[:, 0:1], None, ALU.mult).then_inc(f_w_ready, 1)
                    dve.wait_ge(f_expy_ready, t + 1)
                    nc.vector.scalar_tensor_tensor(elu1[:, 0, :], agg[0][:, 0:D], 0.0, expy[:, 0, :],
                                                   ALU.max, ALU.add).then_inc(f_out_ready, 1)
                    dve.wait_ge(f_out_ready, 2 * t + 1)
                    nc.vector.scalar_tensor_tensor(f_out[:, :], elu1[:, 0, :], -1.0, f_x[:, :],
                                                   ALU.add, ALU.add).then_inc(f_out_ready, 1)
                    dve.wait_ge(f_stored, 16 * (t + 1))
                    stand_apart(dve)
                with dve.Else():
                    dve.sem_inc(fchain, F_CHAIN)
                    dve.sem_inc(f_e_ready, 1)
                    dve.sem_inc(f_w_ready, 2)
                    dve.sem_inc(f_out_ready, 2)

        @block.tensor
        def _(pe):
            pe.wait_ge(consts, PACK + 4)
            pe.wait_ge(w_in, 48)
            nc.tensor.transpose(misc[:, 0:P], w_sb[:, :], ident[:, :]).then_inc(wT_ps_ready, 1)
            pe.wait_ge(wT_ready, 1)
            nc.tensor.matmul(misc[:, P:P + 2], wT[:, :], a_sb[:, :], start=True, stop=True).then_inc(wa_ps_ready, 1)
            pe.wait_ge(wa_ready, 1)

            def transposes(n):
                pe.wait_ge(centered, (n * QT) // XT + 1)
                if n >= 2:
                    pe.wait_ge(relT_ready, n - 1)
                for i in range(QT):
                    last = nc.tensor.transpose(xT_ps[n % 2][:, i * P:(i + 1) * P], xs[:, QT * n + i, :], ident[:, :])
                last.then_inc(xT_ready, 1)

            transposes(0)
            for n in range(NQ):
                if n + 1 < NQ:
                    transposes(n + 1)
                pe.wait_ge(relT_ready, n + 1)
                if n >= 2:
                    pe.wait_ge(h_ready, QT * (n - 1))
                for i in range(QT):
                    lhs = relT[:, n % 2, i * P:(i + 1) * P]
                    nc.tensor.matmul(ds_ps[:, QT * n + i, :], lhs, wa[:, :], start=True, stop=True)
                    last = nc.tensor.matmul(h_ps[n % 2][:, i * D:(i + 1) * D], lhs, w_sb[:, :], start=True, stop=True)
                last.then_inc(h_ps_ready, 1)
            pe.wait_ge(d_ok_ready, 1)
            nc.tensor.transpose(misc[0:NT, 256:256 + P], d_ok[:, :], ident[:, :]).then_inc(dT_ps_ready, 1)
            pe.wait_ge(dT_ready, 1)

            def pack(g, r, more):
                i, half = divmod(r, 2)
                pe.wait_ge(mask_ready, 4 * g + r + 1)
                if half == 0 and more:
                    pe.wait_ge(keys_taken, GT * (g - 1) + i + 1)
                for bk in range(2):
                    bank = packed[2 * i + bk]
                    if half == 0:
                        nc.tensor.matmul(bank[:, :], cell_w[0:2, :], cell_no[0:2, bk * BANK:(bk + 1) * BANK],
                                         start=True, stop=False)
                    for k in range(PACK // 2):
                        c0 = k * CELLS + bk * BANK
                        last = nc.tensor.matmul(bank[:, :], pack_w[:, half * (PACK // 2) + k, :],
                                                mask_ring[:, r, c0:c0 + BANK], start=False,
                                                stop=(half == 1 and k == PACK // 2 - 1))
                last.then_inc(packed_ready, 1)

            def weigh(b, g, u, first):
                for i in range(GT):
                    acc = agg[u][:, i * D:(i + 1) * D]
                    left = pe.value_load(need[i:i + 1, u:u + 1], min_val=0, max_val=SLOTS * PEN)
                    base = (GT * g + i) * SLOTS
                    if i == 0:
                        pe.wait_ge(xh_in[u], 32 * b)
                        if not first:
                            pe.wait_ge(out_ready, g - 1)
                        pe.wait_ge(gathered[u], 16 * GT * SLOTS * b)

                    def rows(k0, k1):
                        for k in range(k0, k1):
                            pe.wait_ge(diag_ready, base + k + 1)
                            nc.tensor.matmul(acc, diag[:, k % DIAG, :], G[:, u, i, k, 0:D], start=(k == 0),
                                             stop=False).then_inc(diag_used, 1)

                    rows(0, DIAG)
                    for k0, k1 in DIAG_STEPS:
                        with pe.If(left < (SLOTS - k0) * PEN):
                            rows(k0, k1)
                        with pe.Else():
                            pe.drain().then_inc(diag_used, k1 - k0)
                    last = nc.tensor.matmul(acc, ident[:, :], h_in[:, u, i, 0:D], start=False, stop=True)
                last.then_inc(agg_ready, 1)

            def emit(b, ahead, behind, first=False):
                for u in range(2):
                    g = 2 * b + u
                    if ahead:
                        for r in range(4):
                            pack(g, r, behind or u)
                    if behind:
                        weigh(b, g - 2, u, first)
                    if ahead:
                        pe.wait_ge(pens_ready, g + 1)
                        if behind or u:
                            pe.wait_ge(need_ready, g)
                        nc.tensor.transpose(small[0:GT, 0:P], pens[:, :], ident[:, :]).then_inc(pensT_ready, 1)

            emit(0, True, False)
            emit(1, True, True, True)
            with pe.Fori(2, NB) as b:
                emit(b, True, True)
            emit(NB, False, True)

            pe.wait_ge(vloop, vloop_end[0])
            nc.tensor.transpose(small[0:NT, 128:128 + P], flag_all[:, :], ident[:, :]).then_inc(flagT_ready, 1)
            pe.wait_ge(flag_col_ready, 1)
            nc.tensor.transpose(small[0:1, 256:256 + NT], f_flag_c[:, :], ident[0:NT, 0:NT]).then_inc(flag_row_ready, 1)

            pe.wait_ge(flags_ready, 1)
            pe.wait_ge(f_const_in, 32)
            with pe.Fori(0, NT) as t:
                flag = pe.value_load(f_flag[0:1, bass.ds(t, 1)], min_val=0, max_val=1)
                with pe.If(flag > 0):
                    pe.wait_ge(f_w_ready, 2 * (t + 1))

                    def f_transposes(c):
                        if c >= 2:
                            pe.wait_ge(f_T_ready, t * F_CHUNKS + c - 1)
                        for i in range(QT):
                            last = nc.tensor.transpose(banks[c % 2][:, i * P:(i + 1) * P],
                                                       f_e[:, (QT * c + i) * P:(QT * c + i + 1) * P], ident[:, :])
                        last.then_inc(f_T_ps_ready, 1)

                    f_transposes(0)
                    for c in range(F_CHUNKS):
                        if c + 1 < F_CHUNKS:
                            f_transposes(c + 1)
                        pe.wait_ge(f_T_ready, t * F_CHUNKS + c + 1)
                        for i in range(QT):
                            nc.tensor.matmul(agg[0][:, 0:D], f_T[:, c % 2, i * P:(i + 1) * P], f_h[:, QT * c + i, 0:D],
                                             start=(c == 0 and i == 0), stop=False)
                    nc.tensor.matmul(agg[0][:, 0:D], ident[:, :], f_h[:, bass.ds(t, 1), 0:D].rearrange("p t d -> p (t d)"),
                                     start=False, stop=True).then_inc(f_agg_ready, 1)
                    pe.wait_ge(f_stored, 16 * (t + 1))
                    stand_apart(pe)
                with pe.Else():
                    pe.sem_inc(f_T_ps_ready, F_CHUNKS)
                    pe.sem_inc(f_agg_ready, 1)


_INS = ["x", "adj", "L0_gnn_W", "L0_gnn_a"]
_OUTS = [((8192, 128), "float32")]


def kernel(**inputs):
    import numpy as _np
    import concourse.bacc as _bacc
    from concourse import mybir as _mybir
    from concourse.bass_utils import run_bass_kernel_spmd as _run

    nc = _bacc.Bacc("TRN2", target_bir_lowering=False, num_devices=1)
    arrays, args = {}, []
    for name in _INS:
        a = _np.ascontiguousarray(inputs[name])
        arrays[f"in_{name}_dram"] = a
        args.append(nc.dram_tensor(f"in_{name}_dram", a.shape, _mybir.dt.from_np(a.dtype), kind="ExternalInput").ap())
    for i, (shape, dtype) in enumerate(_OUTS):
        dt = _mybir.dt.from_np(_np.dtype(dtype))
        args.append(nc.dram_tensor(f"out_{i}_dram", shape, dt, kind="ExternalOutput").ap())
    gat_kernel(nc, *args)
    r = _run(nc, [arrays], core_ids=[0])
    return r.results[0]["out_0_dram"]
```

```python
import concourse.bass as bass
from concourse import mybir
from contextlib import ExitStack

FP32 = mybir.dt.float32
BF16 = mybir.dt.bfloat16
I32 = mybir.dt.int32
ALU = mybir.AluOpType
ACT = mybir.ActivationFunctionType
AX = mybir.AxisListType.X

P = 128
LN_EPS = 1e-5
SLOPE = 0.2
THR = 1e-4
BIG = 1e30
F_BIG = 4e28
VALID_ABOVE = -1e28


def gat_kernel(nc, x, adj, w, a, out):
    N, D = x.shape
    NT = N // P
    HALF = N // 2
    GT = 2
    NG = NT // GT
    NB = NG // 2
    CELLS = 1024
    PACK = N // CELLS
    BANK = 512
    SPLIT = 256
    RUN = 16
    SEGS = 4
    KEYS = 2 * SEGS * 8
    SLOTS = 32
    ROW = D + 1
    QT = 4
    NQ = NT // QT
    NX = 4
    XT = NT // NX
    DIAG = 8
    EXP_OFF = (127 + 10) * CELLS
    PEN = 1 << 20
    EXP_MASK = 0x7F800000

    table = nc.dram_tensor("table", (N, ROW), FP32, kind="Internal").ap()
    d_line = nc.dram_tensor("d_line", (N // P, P), FP32, kind="Internal").ap()

    x_t = x.rearrange("(t p) d -> p t d", p=P)
    out_t = out.rearrange("(t p) d -> p t d", p=P)
    table_t = table.rearrange("(t p) r -> p t r", p=P)
    adj_t = adj.rearrange("(t p) (h c) -> p t h c", p=P, h=2)
    adj_q = adj.rearrange("(t p) (q c) -> p t q c", p=P, q=4)

    ctx = ExitStack()
    with ctx:
        def sb(name, shape, dt):
            return ctx.enter_context(nc.sbuf_tensor(name, shape, dt))

        def pb(name, shape, dt=FP32):
            return ctx.enter_context(nc.psum_tensor(name, shape, dt))

        def sem(name):
            return ctx.enter_context(nc.semaphore(name))

        adj_ring = sb("adj_ring", [P, 4, HALF], I32)
        mask_ring = sb("mask_ring", [P, 4, HALF], BF16)
        gbuf = sb("gbuf", [P, 2 * GT * SLOTS * ROW], FP32)
        G = gbuf[:, :].rearrange("p (b i k r) -> p b i k r", b=2, i=GT, k=SLOTS)
        ident = sb("ident", [P, P], FP32)
        pack_w = sb("pack_w", [P, PACK, P], BF16)
        cell_no = sb("cell_no", [2, CELLS], BF16)
        cell_w = sb("cell_w", [2, P], BF16)
        s_all = sb("s_all", [P, NT], FP32)
        flag_all = sb("flag_all", [P, NT], FP32)
        V = sb("V", [P, GT, 2, KEYS], FP32)
        kint = sb("kint", [P, GT, KEYS], I32)
        cell = sb("cell", [P, GT, KEYS], I32)
        hib = sb("hib", [P, GT, 2, KEYS], I32)
        expo = sb("expo", [P, GT, 2, KEYS], I32)
        cand = sb("cand", [P, GT, 2, KEYS], FP32)
        rest = sb("rest", [P, GT, KEYS], FP32)
        mx = sb("mx", [P, 4, GT], FP32)
        top = sb("top", [P, GT, SLOTS], FP32)
        pen = sb("pen", [P, 2, GT, SLOTS], FP32)
        idx = sb("idx", [P, 2, GT, SLOTS], I32)
        pens = sb("pens", [P, GT], FP32)
        need = sb("need", [GT, 2], I32)
        xm = sb("xm", [P, GT, SLOTS], FP32)
        e = sb("e", [P, GT, SLOTS], FP32)
        em = sb("em", [P, GT, SLOTS], FP32)
        q = sb("q", [P, GT, SLOTS], FP32)
        att = sb("att", [P, GT, SLOTS], FP32)
        keep = sb("keep", [P, GT, SLOTS], FP32)
        valid = sb("valid", [P, GT, SLOTS], FP32)
        wts = sb("wts", [P, GT, SLOTS], FP32)
        r_max = sb("r_max", [P, GT], FP32)
        r_sum = sb("r_sum", [P, GT], FP32)
        r_inv = sb("r_inv", [P, GT], FP32)
        r_deg = sb("r_deg", [P, GT], FP32)
        r_gain = sb("r_gain", [P, GT], FP32)
        diag = sb("diag", [P, DIAG, P], FP32)
        x_in = sb("x_in", [P, 2, GT, D], FP32)
        h_in = sb("h_in", [P, 2, GT, ROW], FP32)
        negy = sb("negy", [P, GT, D], FP32)
        expy = sb("expy", [P, GT, D], FP32)
        elu1 = sb("elu1", [P, GT, D], FP32)
        out_sb = sb("out_sb", [P, 2, GT, D], FP32)

        banks = [pb(f"bank{i}", [P, BANK]) for i in range(8)]
        packed = banks[0:4]
        agg = banks[4:6]
        small = banks[6]
        pensT = small[0:GT, 256:256 + P]

        xs = gbuf[:, 0:NT * D].rearrange("p (t d) -> p t d", d=D)
        ts = gbuf[:, NT * D:NT * D + NT * ROW].rearrange("p (t r) -> p t r", r=ROW)
        w_sb = sb("w_sb", [P, D], FP32)
        a_sb = sb("a_sb", [P, 3], FP32)
        wT = sb("wT", [P, P], FP32)
        wa = sb("wa", [P, 3], FP32)
        center = sb("center", [P, P], FP32)
        mean_w = sb("mean_w", [P, 1], FP32)
        std = sb("std", [P, NT], FP32)
        rstd = sb("rstd", [P, NT], FP32)
        hz = sb("hz", [P, NT], FP32)
        d_raw = sb("d_raw", [P, NT], FP32)
        d_ok = sb("d_ok", [P, NT], FP32)
        dT = sb("dT", [NT, P], FP32)
        eps = sb("eps", [P, 1], FP32)
        xT = sb("xT", [P, QT * P], FP32)
        relT = sb("relT", [P, QT * P], FP32)
        sqT = sb("sqT", [P, QT * P], FP32)
        xT_ps, xc_ps, h_ps, misc = banks[4], banks[5], banks[7], banks[7]
        ds_ps = small[:, 0:3 * NT].rearrange("p (t c) -> p t c", c=3)
        var_ps = small[:, 3 * NT:4 * NT]

        FQ = 4
        f_adj = adj_ring[:, 0:2, :].rearrange("p h c -> p (h c)").rearrange("p (q c) -> p q c", q=FQ)
        f_z = f_adj.bitcast(FP32)
        f_e = adj_ring[:, 2:4, :].rearrange("p h c -> p (h c)").bitcast(FP32).rearrange("p (q c) -> p q c", q=FQ)
        f_d = mask_ring[:, :, :].rearrange("p r c -> p (r c)").bitcast(FP32).rearrange("p (q c) -> p q c", q=FQ)
        f_h = G[:, 0, :, :, :].rearrange("p i k r -> p (i k) r")
        f_rest = GT * SLOTS * ROW
        f_T = gbuf[:, f_rest:f_rest + 2 * BANK].rearrange("p (b c) -> p b c", b=2)
        f_sign = gbuf[:, f_rest + 2 * BANK:f_rest + 2 * BANK + N // FQ]
        f_flag_c = sb("f_flag_c", [NT, 1], FP32)
        f_order = sb("f_order", [1, NT], FP32)
        f_keys = sb("f_keys", [1, NT], FP32)
        f_sorted = sb("f_sorted", [1, NT], FP32)
        f_list = sb("f_list", [1, NT + 1], I32)
        f_counted = sb("f_counted", [1, 1], FP32)
        f_count = sb("f_count", [1, 1], I32)
        f_x = sb("f_x", [P, D], FP32)
        f_y = sb("f_y", [P, D], FP32)
        f_out = sb("f_out", [P, D], FP32)
        f_far = sb("f_far", [P, 1], FP32)
        f_big = sb("f_big", [P, 1], FP32)
        f_max = sb("f_max", [P, FQ], FP32)
        f_sum = sb("f_sum", [P, FQ], FP32)
        f_signs = sb("f_signs", [P, FQ], FP32)
        f_row = sb("f_row", [P, 11], FP32)

        ident0 = sem("ident0")
        consts = sem("consts")
        w_in = sem("w_in")
        x_loaded = [sem(f"x_loaded{c}") for c in range(NX)]
        vchain = sem("vchain")
        vloop = sem("vloop")
        std_ready = sem("std_ready")
        rstd_ready = sem("rstd_ready")
        scaled = sem("scaled")
        xT_ps_ready = sem("xT_ps_ready")
        xT_ready = sem("xT_ready")
        xc_ready = sem("xc_ready")
        sqT_ready = sem("sqT_ready")
        wT_ps_ready = sem("wT_ps_ready")
        wT_ready = sem("wT_ready")
        wa_ps_ready = sem("wa_ps_ready")
        wa_ready = sem("wa_ready")
        relT_ready = sem("relT_ready")
        h_ps_ready = sem("h_ps_ready")
        h_ready = sem("h_ready")
        d_ok_ready = sem("d_ok_ready")
        dT_ps_ready = sem("dT_ps_ready")
        dT_ready = sem("dT_ready")
        table_stored = sem("table_stored")
        d_stored = sem("d_stored")

        adj_in = [sem(f"adj_in{r}") for r in range(4)]
        wait_passed = sem("wait_passed")
        mask_ready = sem("mask_ready")
        mask0_ready = sem("mask0_ready")
        relu0_ready = sem("relu0_ready")
        packed_ready = sem("packed_ready")
        keys_taken = sem("keys_taken")
        idx_ready = sem("idx_ready")
        pens_ready = sem("pens_ready")
        pensT_ready = sem("pensT_ready")
        need_ready = sem("need_ready")
        gathered = [sem(f"gathered{u}") for u in range(2)]
        em_ready = sem("em_ready")
        q_ready = sem("q_ready")
        wts_ready = sem("wts_ready")
        diag_ready = sem("diag_ready")
        diag_used = sem("diag_used")
        xh_in = [sem(f"xh_in{u}") for u in range(2)]
        agg_ready = sem("agg_ready")
        negy_ready = sem("negy_ready")
        expy_ready = sem("expy_ready")
        out_ready = sem("out_ready")
        out_stored = [sem(f"out_stored{u}") for u in range(2)]

        flagT_ready = sem("flagT_ready")
        flag_col_ready = sem("flag_col_ready")
        flag_row_ready = sem("flag_row_ready")
        flags_ready = sem("flags_ready")
        f_d_in = sem("f_d_in")
        f_h_in = sem("f_h_in")
        f_in = [sem(f"f_in{c}") for c in range(FQ)]
        f_x_in = sem("f_x_in")
        fchain = sem("fchain")
        f_pen_ready = sem("f_pen_ready")
        f_d_ready = sem("f_d_ready")
        f_z_ready = sem("f_z_ready")
        f_signs_ready = sem("f_signs_ready")
        f_m_ready = sem("f_m_ready")
        f_e_ready = sem("f_e_ready")
        f_y_ready = sem("f_y_ready")
        f_least_ready = sem("f_least_ready")
        f_scale_ready = sem("f_scale_ready")
        f_q_ready = sem("f_q_ready")
        f_w_ready = sem("f_w_ready")
        f_T_ps_ready = sem("f_T_ps_ready")
        f_T_ready = sem("f_T_ready")
        f_T_used = sem("f_T_used")
        f_negy_ready = sem("f_negy_ready")
        f_expy_ready = sem("f_expy_ready")
        f_out_ready = sem("f_out_ready")
        f_stored = sem("f_stored")

        GATHER_STEPS = [(4, 6), (6, 7), (7, 8), (8, 9), (9, 10), (10, 12), (12, 16), (16, 24), (24, SLOTS)]
        DIAG_STEPS = [(DIAG, 12), (12, 16), (16, SLOTS)]

        NODE_STEPS = [range(NQ - 12, NQ - 6), range(NQ - 6, NQ)]

        F_CHUNKS = N // BANK
        F_CHAIN = 8
        F_BLOCK = 9
        assert (NT - 1) % F_BLOCK == 0

        def wait_mask(eng, g, r):
            if r == 0:
                eng.wait_ge(mask0_ready, g + 1)
            else:
                eng.wait_ge(mask_ready, 3 * g + r)

        class Order:

            def __init__(self, eng, s, base=0):
                self.eng, self.s, self.base, self.n = eng, s, base, 0

            def then(self, ins):
                ins.then_inc(self.s, 1)
                self.n += 1

            def settle(self, apart=False):
                self.eng.wait_ge(self.s, self.base + self.n)
                if apart:
                    stand_apart(self.eng)

        CONSTS = PACK + 11
        def stand_apart(eng):
            eng.sem_inc(wait_passed, 1)

        def for_other_flagged(eng, count, work):
            with eng.If(count > 1):
                with eng.Fori(0, (NT - 1) // F_BLOCK) as jb:
                    with eng.If(count > jb * F_BLOCK + 1):
                        with eng.Fori(0, F_BLOCK) as ji:
                            with eng.If(count > jb * F_BLOCK + ji + 1):
                                work(jb * F_BLOCK + ji + 1)

        block = ctx.enter_context(nc.Block())

        @block.sync
        def _(sp):
            sp.dma_start(w_sb[:, :], w[:, :]).then_inc(w_in, 16)
            for c in range(2):
                sp.dma_start(a_sb[:, c:c + 1], a[c * D:(c + 1) * D, :]).then_inc(w_in, 16)
            for c in range(NX):
                sp.dma_start(xs[:, c * XT:(c + 1) * XT, :], x_t[:, c * XT:(c + 1) * XT, :]).then_inc(x_loaded[c], 16)
            for r in range(4):
                sp.dma_start(adj_ring[:, r, :], adj_t[:, r // 2, r % 2, :]).then_inc(adj_in[r], 16)
            def adj_loads(g, last):
                if last:
                    return
                for r in range(4):
                    wait_mask(sp, g, r)
                    sp.dma_start(adj_ring[:, r, :], adj_t[:, GT * (g + 1) + r // 2, r % 2, :]).then_inc(adj_in[r], 16)

            def body(b, ahead, behind, final):
                for u in range(2):
                    g = 2 * b + u
                    if ahead:
                        adj_loads(g, final and u == 1)
                    if isinstance(g, int) and g == 1:
                        sp.wait_ge(scaled, NX)
                        sp.wait_ge(d_ok_ready, 2)
                        sp.dma_start(table_t, ts).then_inc(table_stored, 16)
                        sp.wait_ge(dT_ready, 1)
                        sp.dma_start(d_line, dT[:, :]).then_inc(d_stored, 16)
                        sp.wait_ge(table_stored, 16)
                    if behind:
                        sp.wait_ge(out_ready, g - 2 + 1)
                        sp.dma_start(out_t[:, bass.ds(GT * (g - 2), GT), :], out_sb[:, u, :, :]).then_inc(out_stored[u], 16)
                    own = [(g, u)] if ahead else []
                    if not behind:
                        own = [(0, 0), (1, 1)] if u else []
                    for gg, uu in own:
                        sp.dma_start(x_in[:, uu, :, :], x_t[:, bass.ds(GT * gg, GT), :]).then_inc(xh_in[uu], 16)
                        sp.dma_start(h_in[:, uu, :, :], table_t[:, bass.ds(GT * gg, GT), :]).then_inc(xh_in[uu], 16)

            def f_tile(j):
                t = sp.value_load(f_list[0:1, bass.ds(j, 1)], min_val=0, max_val=NT - 1)
                sp.dma_start(f_x[:, :], x_t[:, t, :]).then_inc(f_x_in, 16)
                with sp.If(count > j + 1):
                    f_loads(j + 1)
                sp.wait_ge(f_out_ready, 2 * (j + 1))
                sp.dma_start(out_t[:, t, :], f_out[:, :]).then_inc(f_stored, 16)
                sp.wait_ge(f_stored, 16 * (j + 1))
                stand_apart(sp)

            body(0, True, False, False)
            with sp.Fori(1, NB - 1) as b:
                body(b, True, True, False)
            body(NB - 1, True, True, True)

            sp.wait_ge(packed_ready, 4 * NG)
            sp.wait_ge(d_stored, 16)
            sp.dma_start(mask_ring[:, :, :].rearrange("p r c -> p (r c)").bitcast(FP32),
                         d_line.rearrange("(o t) p -> o (t p)", o=1).to_broadcast([P, N])).then_inc(f_d_in, 16)
            sp.wait_ge(flags_ready, 1)
            count = sp.value_load(f_count[0:1, 0:1], min_val=0, max_val=NT)

            def f_loads(j):
                t = sp.value_load(f_list[0:1, bass.ds(j, 1)], min_val=0, max_val=NT - 1)
                for c in range(FQ):
                    if not (isinstance(j, int) and j == 0):
                        sp.wait_ge(f_signs_ready, (j - 1) * FQ + c + 1)
                        sp.wait_ge(f_e_ready, (j - 1) * FQ + c + 1)
                    sp.dma_start(f_adj[:, c, :], adj_q[:, t, c, :]).then_inc(f_in[c], 16)

            with sp.If(count > 0):
                f_loads(0)
            sp.wait_ge(agg_ready, NG - 1)
            sp.dma_start(f_h, table_t).then_inc(f_h_in, 16)
            body(NB, False, True, False)
            for u in range(2):
                sp.wait_ge(out_stored[u], 16 * NB)

            with sp.If(count > 0):
                f_tile(0)
            for_other_flagged(sp, count, f_tile)
            sp.wait_ge(f_d_in, 16)
            sp.wait_ge(f_h_in, 16)

        @block.gpsimd
        def _(pool):
            pool.memset(ident[:, :], 0.0).then_inc(ident0, 1)
            pool.memset(pack_w[:, :, :], 0.0).then_inc(ident0, 1)
            pool.memset(center[:, :], -1.0 / D).then_inc(ident0, 1)
            pool.memset(eps[:, :], LN_EPS).then_inc(consts, 1)
            pool.memset(mean_w[:, :], 1.0 / D).then_inc(consts, 1)
            pool.memset(a_sb[:, 2:3], 1.0).then_inc(consts, 1)
            pool.iota(f_order[:, :], pattern=[[-1, NT]], base=NT, channel_multiplier=0,
                      allow_small_or_imprecise_dtypes=True).then_inc(consts, 1)
            pool.memset(f_far[:, :], -VALID_ABOVE).then_inc(consts, 1)
            pool.memset(f_big[:, :], F_BIG).then_inc(consts, 1)
            pool.wait_ge(ident0, 3)
            pool.affine_select(out=center[:, :], in_=center[:, :], compare_op=ALU.not_equal, fill=1.0 - 1.0 / D,
                               base=0, pattern=[[-1, P]], channel_multiplier=1).then_inc(consts, 1)
            pool.affine_select(out=ident[:, :], in_=ident[:, :], compare_op=ALU.not_equal, fill=1.0, base=0,
                               pattern=[[-1, P]], channel_multiplier=1).then_inc(consts, 1)
            for k in range(PACK):
                pool.affine_select(out=pack_w[:, k, :], in_=pack_w[:, k, :], compare_op=ALU.not_equal,
                                   fill=float(CELLS << k), base=0, pattern=[[-1, P]],
                                   channel_multiplier=1).then_inc(consts, 1)
            pool.iota(cell_no[0:2, :].rearrange("p (a c) -> p a c", c=256), pattern=[[0, CELLS // 256], [1, 256]],
                      base=0, channel_multiplier=0, allow_small_or_imprecise_dtypes=True).then_inc(ident0, 1)
            pool.memset(cell_w[0:2, :], 1.0).then_inc(ident0, 1)
            pool.wait_ge(ident0, 5)
            pool.iota(cell_no[0:1, :].rearrange("p (a c) -> p a c", c=256), pattern=[[1, CELLS // 256], [0, 256]],
                      base=0, channel_multiplier=0, allow_small_or_imprecise_dtypes=True).then_inc(consts, 1)
            pool.memset(cell_w[0:1, :], 256.0).then_inc(consts, 1)

            pool.memset(gbuf[:, NT * (D + ROW):], 0.0).then_inc(consts, 1)
            for c in range(NX):
                cs = slice(c * XT, (c + 1) * XT)
                pool.wait_ge(rstd_ready, c + 1)
                pool.wait_ge(h_ready, (c + 1) * XT // QT)
                pool.tensor_tensor(ts[:, cs, 0:D], ts[:, cs, 0:D],
                                   rstd[:, cs].unsqueeze(2).to_broadcast([P, XT, D]), ALU.mult).then_inc(scaled, 1)
            pool.wait_ge(table_stored, 16)

            def emit(b, ahead, behind):
                if not ahead:
                    return
                for u in range(2):
                    g = 2 * b + u
                    pool.wait_ge(need_ready, g + 1)
                    pool.wait_ge(idx_ready, g + 1)
                    if behind:
                        pool.wait_ge(agg_ready, g - 1)
                    stand_apart(pool)
                    for i in range(GT):
                        left = pool.value_load(need[i:i + 1, u:u + 1], min_val=0, max_val=SLOTS * PEN)

                        def gather(k):
                            pool.indirect_dma_start(
                                out=G[:, u, i, k, :], out_offset=None, in_=table[:, :],
                                in_offset=bass.IndirectOffsetOnAxis(ap=idx[:, u, i, k:k + 1], axis=0),
                                bounds_check=N - 1, oob_is_err=False).then_inc(gathered[u], 16)

                        for k in range(GATHER_STEPS[0][0]):
                            gather(k)
                        for k0, k1 in GATHER_STEPS:
                            with pool.If(left < (SLOTS - k0) * PEN):
                                for k in range(k0, k1):
                                    gather(k)
                            with pool.Else():
                                pool.inc_swdge_sem([gathered[u]], [16 * (k1 - k0)])

            emit(0, True, False)
            with pool.Fori(1, NB) as b:
                emit(b, True, True)
        @block.scalar
        def _(act):
            act.wait_ge(consts, CONSTS)

            def node_step(n):
                if n < NQ:
                    act.wait_ge(xT_ps_ready, n + 1)
                    if n:
                        act.wait_ge(xc_ready, n)
                    nc.scalar.activation(xT[:, :], xT_ps[:, :], ACT.Copy).then_inc(xT_ready, 1)
                if n:
                    act.wait_ge(h_ps_ready, n)
                    nc.scalar.activation(ts[:, QT * (n - 1):QT * n, 0:D], h_ps[:, :].rearrange("p (t d) -> p t d", t=QT),
                                         ACT.Copy).then_inc(h_ready, 1)
                    if n % (NQ // NX) == 0:
                        c = n // (NQ // NX)
                        nc.scalar.activation(std[:, (c - 1) * XT:c * XT], var_ps[:, (c - 1) * XT:c * XT], ACT.Sqrt,
                                             bias=eps[:, 0:1]).then_inc(std_ready, 1)
                if n < NQ:
                    act.wait_ge(xc_ready, n + 1)
                    if n:
                        act.wait_ge(h_ps_ready, n)
                    nc.scalar.activation(sqT[:, :], xc_ps[:, :], ACT.Square).then_inc(sqT_ready, 1)

            def make_mask0(g, more):
                act.wait_ge(adj_in[0], 16 * (g + 1))
                if more:
                    act.wait_ge(packed_ready, 4 * (g - 1) + 1)
                nc.scalar.activation(mask_ring[:, 0, :], adj_ring[:, 0, :], ACT.Relu).then_inc(relu0_ready, 1)
                act.wait_ge(relu0_ready, g + 1)
                nc.scalar.activation(mask_ring[:, 0, :], mask_ring[:, 0, :], ACT.Sign).then_inc(mask0_ready, 1)

            def finish_group(b, g, u, first=False):
                act.wait_ge(em_ready, g + 1)
                nc.scalar.activation(q[:, :, :], em[:, :, :], ACT.Exp).then_inc(q_ready, 1)
                act.wait_ge(wts_ready, g + 1)
                stand_apart(act)
                for i in range(GT):
                    left = act.value_load(need[i:i + 1, u:u + 1], min_val=0, max_val=SLOTS * PEN)
                    base = (GT * g + i) * SLOTS

                    def diagonals(k0, k1):
                        for k in range(k0, k1):
                            if first and i == 0 and u == 0 and k < DIAG:
                                pass
                            else:
                                act.wait_ge(diag_used, base + k - DIAG + 1)
                            nc.scalar.activation(diag[:, k % DIAG, :], ident[:, :], ACT.Copy,
                                                 scale=wts[:, i, k:k + 1]).then_inc(diag_ready, 1)

                    diagonals(0, DIAG)
                    for k0, k1 in DIAG_STEPS:
                        with act.If(left < (SLOTS - k0) * PEN):
                            diagonals(k0, k1)
                        with act.Else():
                            act.drain().then_inc(diag_ready, k1 - k0)
                act.wait_ge(agg_ready, g + 1)
                y = agg[u][:, 0:GT * D].rearrange("p (i d) -> p i d", i=GT)
                nc.scalar.activation(negy[:, :, :], y, ACT.Relu, scale=-1.0).then_inc(negy_ready, 1)
                act.wait_ge(negy_ready, g + 1)
                if not first or u:
                    act.wait_ge(out_ready, g)
                nc.scalar.activation(expy[:, :, :], negy[:, :, :], ACT.Exp, scale=-1.0).then_inc(expy_ready, 1)

            def emit(b, ahead, behind):
                for u in range(2):
                    if ahead:
                        make_mask0(2 * b + u, behind or u)
                    if not behind:
                        for n in NODE_STEPS[u]:
                            node_step(n)
                        if u:
                            node_step(NQ)
                        continue
                    finish_group(b, 2 * b + u - 2, u, behind == "first")

            for n in range(NODE_STEPS[0][0]):
                node_step(n)
            emit(0, True, False)
            emit(1, True, "first")
            with act.Fori(2, NB) as b:
                emit(b, True, True)

            def f_scores(j):
                t = act.value_load(f_list[0:1, bass.ds(j, 1)], min_val=0, max_val=NT - 1)
                for c in range(FQ):
                    act.wait_ge(f_in[c], 16 * (j + 1))
                    if c == 0 and not isinstance(j, int):
                        act.wait_ge(f_T_ps_ready, j * F_CHUNKS)
                    stand_apart(act)
                    nc.scalar.activation(f_e[:, c, :], f_adj[:, c, :], ACT.Relu, scale=-F_BIG,
                                         bias=f_big[:, 0:1]).then_inc(f_pen_ready, 1)
                for c in range(FQ):
                    act.wait_ge(f_d_ready, j * FQ + c + 1)
                    stand_apart(act)
                    nc.scalar.activation(f_z[:, c, :], f_e[:, c, :], ACT.Identity,
                                         bias=s_all[:, bass.ds(t, 1)]).then_inc(f_z_ready, 1)
                act.wait_ge(f_m_ready, j + 1)
                for c in range(FQ):
                    act.wait_ge(f_e_ready, j * FQ + c + 1)
                    nc.scalar.activation(f_e[:, c, :], f_e[:, c, :], ACT.Exp, bias=f_row[:, 0:1],
                                         accum_out=f_sum[:, c:c + 1]).then_inc(f_q_ready, 1)

            def f_sums(j):
                def signs(c):
                    act.wait_ge(f_z_ready, j * FQ + c + 1)
                    if c:
                        act.wait_ge(f_signs_ready, j * FQ + c)
                    nc.scalar.activation(f_sign, f_z[:, c, :], ACT.Sign, bias=f_far[:, 0:1],
                                         accum_out=f_signs[:, c:c + 1]).then_inc(f_signs_ready, 1)

                for c in range(FQ):
                    signs(c)
                for c in range(F_CHUNKS):
                    act.wait_ge(f_T_ps_ready, j * F_CHUNKS + c + 1)
                    if c >= 2:
                        act.wait_ge(f_T_used, j * F_CHUNKS + c - 1)
                    nc.scalar.activation(f_T[:, c % 2, :], banks[c % 2][:, :], ACT.Copy).then_inc(f_T_ready, 1)
                act.wait_ge(f_y_ready, j + 1)
                nc.scalar.activation(negy[:, 0, :], f_y[:, :], ACT.Relu, scale=-1.0).then_inc(f_negy_ready, 1)
                act.wait_ge(f_negy_ready, j + 1)
                nc.scalar.activation(expy[:, 0, :], negy[:, 0, :], ACT.Exp, scale=-1.0).then_inc(f_expy_ready, 1)

            def f_tile(j):
                f_scores(j)
                f_sums(j)

            finish_group(NB, NG - 2, 0)
            act.wait_ge(flags_ready, 1)
            count = act.value_load(f_count[0:1, 0:1], min_val=0, max_val=NT)
            with act.If(count > 0):
                f_scores(0)
            finish_group(NB, NG - 1, 1)
            with act.If(count > 0):
                f_sums(0)
            for_other_flagged(act, count, f_tile)

        @block.vector
        def _(dve):
            v = Order(dve, vchain)
            dve.wait_ge(wT_ps_ready, 1)
            nc.vector.tensor_copy(wT[:, :], misc[:, 0:P]).then_inc(wT_ready, 1)
            dve.wait_ge(wa_ps_ready, 1)
            nc.vector.tensor_copy(wa[:, :], misc[:, P:P + 3]).then_inc(wa_ready, 1)

            def node_step(n):
                dve.wait_ge(sqT_ready, n + 1)
                if n:
                    dve.wait_ge(h_ps_ready, n)
                nc.vector.tensor_scalar(relT[:, :], xc_ps[:, :], 0.0, None, ALU.max).then_inc(relT_ready, 1)
                if n % (NQ // NX) == 1 and n > 1:
                    inverse_std(n // (NQ // NX) - 1)

            def inverse_std(c):
                dve.wait_ge(std_ready, c + 1)
                nc.vector.reciprocal(rstd[:, c * XT:(c + 1) * XT], std[:, c * XT:(c + 1) * XT]).then_inc(rstd_ready, 1)

            def node_scores():
                inverse_std(NX - 1)
                v.then(nc.vector.tensor_scalar(hz[:, :], ds_ps[:, :, 2], 0.0, -BIG, ALU.is_equal, ALU.mult))
                dve.wait_ge(rstd_ready, NX)
                v.then(nc.vector.tensor_tensor(s_all[:, :], ds_ps[:, :, 0], rstd[:, :], ALU.mult))
                v.then(nc.vector.tensor_tensor(d_raw[:, :], ds_ps[:, :, 1], rstd[:, :], ALU.mult))
                v.settle()
                nc.vector.tensor_tensor(d_ok[:, :], d_raw[:, :], hz[:, :], ALU.add).then_inc(d_ok_ready, 1)
                dve.wait_ge(d_ok_ready, 1)
                nc.vector.tensor_copy(ts[:, :, D], d_ok[:, :]).then_inc(d_ok_ready, 1)
                dve.wait_ge(dT_ps_ready, 1)
                nc.vector.tensor_copy(dT[:, :], misc[0:NT, 0:P]).then_inc(dT_ready, 1)

            def make_mask(g, r, behind):
                dve.wait_ge(adj_in[r], 16 * (g + 1))
                if behind:
                    dve.wait_ge(packed_ready, 4 * (g - 1) + r + 1)
                nc.vector.tensor_scalar(mask_ring[:, r, :], adj_ring[:, r, :], 0, None, ALU.is_gt).then_inc(mask_ready, 1)

            def take_keys(g, i, o):
                dve.wait_ge(packed_ready, 4 * g + 2 * i + 2)
                stand_apart(dve)
                for bk in range(2):
                    segs = packed[2 * i + bk][:, :].rearrange("p (a s r) -> p s a r", s=SEGS, r=RUN)
                    for n in range(SEGS):
                        k0 = (bk * SEGS + n) * 8
                        last = nc.vector.max(V[:, i, 0, k0:k0 + 8], segs[:, n, :, :])
                last.then_inc(keys_taken, 1)

            def decode(g, u, o):
                o.settle()
                dve.wait_ge(keys_taken, GT * (g + 1))
                o.then(nc.vector.tensor_copy(kint[:, :, :], V[:, :, 0, :]))
                o.then(nc.vector.tensor_scalar(hib[:, :, 0, :], V[:, :, 0, :].bitcast(I32), EXP_MASK, None, ALU.bitwise_and))
                o.settle()
                o.then(nc.vector.tensor_scalar(cell[:, :, :], kint[:, :, :], CELLS - 1, None, ALU.bitwise_and))
                o.then(nc.vector.tensor_tensor(V[:, :, 1, :], V[:, :, 0, :], hib[:, :, 0, :].bitcast(FP32), ALU.subtract))
                o.settle()
                o.then(nc.vector.tensor_scalar(expo[:, :, :, :], V[:, :, :, :].bitcast(I32), 23, None, ALU.logical_shift_right))
                o.then(nc.vector.tensor_scalar(hib[:, :, 1, :], V[:, :, 1, :].bitcast(I32), EXP_MASK, None, ALU.bitwise_and))
                o.settle()
                for level in range(2):
                    o.then(nc.vector.scalar_tensor_tensor(cand[:, :, level, :], expo[:, :, level, :], float(CELLS),
                                                          cell[:, :, :], ALU.mult, ALU.add))
                o.then(nc.vector.tensor_tensor(rest[:, :, :], V[:, :, 1, :], hib[:, :, 1, :].bitcast(FP32), ALU.subtract))
                o.settle(apart=True)
                flat = [cand[:, i, :, :].rearrange("p l k -> p (l k)") for i in range(GT)]
                for k in range(0, SLOTS, 8):
                    for i in range(GT):
                        o.then(nc.vector.max(top[:, i, k:k + 8], flat[i]))
                    if k == 0:
                        o.then(nc.vector.tensor_reduce(mx[:, 0, :], rest[:, :, :], AX, ALU.max))
                    if k == 8:
                        o.then(nc.vector.tensor_reduce(mx[:, 1, :], V[:, :, 0, 7:KEYS:8], AX, ALU.max))
                    if k == 16:
                        o.then(nc.vector.tensor_tensor(mx[:, 2, :], mx[:, 0, :], mx[:, 1, :], ALU.max))
                    o.settle(apart=True)
                    if k + 8 < SLOTS:
                        for i in range(GT):
                            o.then(nc.vector.match_replace(out=flat[i], in_to_replace=top[:, i, k:k + 8],
                                                           in_values=flat[i], imm_value=0.0))
                        if k == 16:
                            o.then(nc.vector.tensor_scalar(mx[:, 3, :], mx[:, 2, :], float(CELLS), None, ALU.is_ge))
                        o.settle(apart=True)
                o.then(nc.vector.tensor_scalar(pen[:, u, :, :], top[:, :, :], float(EXP_OFF), float(PEN), ALU.is_lt, ALU.mult))
                o.then(nc.vector.scalar_tensor_tensor(flag_all[:, bass.ds(GT * g, GT)], top[:, :, SLOTS - 1], float(EXP_OFF),
                                                      mx[:, 3, :], ALU.is_ge, ALU.max))
                o.settle()
                nc.vector.tensor_reduce(pens[:, :], pen[:, u, :, :], AX, ALU.add).then_inc(pens_ready, 1)
                nc.vector.scalar_tensor_tensor(idx[:, u, :, :], top[:, :, :], float(-EXP_OFF), pen[:, u, :, :],
                                               ALU.add, ALU.add).then_inc(idx_ready, 1)

            def scores(b, g, u, o):
                dve.wait_ge(gathered[u], 16 * GT * SLOTS * b)
                o.then(nc.vector.scalar_tensor_tensor(xm[:, :, :], pen[:, u, :, :], -BIG / PEN, G[:, u, :, :, D],
                                                      ALU.mult, ALU.add))
                o.settle()
                o.then(nc.vector.tensor_tensor(att[:, :, :], xm[:, :, :],
                                               s_all[:, bass.ds(GT * g, GT)].unsqueeze(2).to_broadcast([P, GT, SLOTS]),
                                               ALU.add))
                o.settle()
                o.then(nc.vector.scalar_tensor_tensor(e[:, :, :], att[:, :, :], SLOPE, att[:, :, :], ALU.mult, ALU.max))
                o.settle()
                o.then(nc.vector.tensor_reduce(r_max[:, :], e[:, :, :], AX, ALU.max))
                o.then(nc.vector.tensor_scalar(valid[:, :, :], e[:, :, :], VALID_ABOVE, None, ALU.is_gt))
                o.settle()
                nc.vector.tensor_tensor(em[:, :, :], e[:, :, :], r_max[:, :].unsqueeze(2).to_broadcast([P, GT, SLOTS]),
                                        ALU.subtract).then_inc(em_ready, 1)
                o.then(nc.vector.tensor_reduce(r_deg[:, :], valid[:, :, :], AX, ALU.add))

            def weights(g, u, o, first):
                dve.wait_ge(q_ready, g + 1)
                o.then(nc.vector.tensor_reduce(r_sum[:, :], q[:, :, :], AX, ALU.add))
                o.settle()
                o.then(nc.vector.reciprocal(r_inv[:, :], r_sum[:, :]))
                o.settle()
                o.then(nc.vector.tensor_tensor(att[:, :, :], q[:, :, :],
                                               r_inv[:, :].unsqueeze(2).to_broadcast([P, GT, SLOTS]), ALU.mult))
                o.then(nc.vector.scalar_tensor_tensor(r_gain[:, :], r_inv[:, :], THR, r_deg[:, :], ALU.is_gt, ALU.mult))
                o.settle()
                o.then(nc.vector.scalar_tensor_tensor(keep[:, :, :], att[:, :, :], THR, att[:, :, :], ALU.is_ge, ALU.mult))
                o.settle()
                nc.vector.tensor_tensor(wts[:, :, :], keep[:, :, :],
                                        r_gain[:, :].unsqueeze(2).to_broadcast([P, GT, SLOTS]), ALU.mult).then_inc(wts_ready, 1)

            def finish(b, g, u, o):
                dve.wait_ge(expy_ready, g + 1)
                dve.wait_ge(xh_in[u], 32 * b)
                y = agg[u][:, 0:GT * D].rearrange("p (i d) -> p i d", i=GT)
                o.then(nc.vector.scalar_tensor_tensor(elu1[:, :, :], y, 0.0, expy[:, :, :], ALU.max, ALU.add))
                o.settle()
                if not (isinstance(b, int) and b == 1):
                    dve.wait_ge(out_stored[u], 16 * (b - 1))
                nc.vector.scalar_tensor_tensor(out_sb[:, u, :, :], elu1[:, :, :], -1.0, x_in[:, u, :, :],
                                               ALU.add, ALU.add).then_inc(out_ready, 1)

            def emit(b, ahead, behind, o):
                for u in range(2):
                    g = 2 * b + u
                    more = behind or u
                    nodes = [] if behind else list(NODE_STEPS[u])

                    def between():
                        if nodes:
                            node_step(nodes.pop(0))

                    if ahead:
                        make_mask(g, 1, more)
                        between()
                    if behind:
                        scores(b, g - 2, u, o)
                    if ahead:
                        make_mask(g, 2, more)
                        between()
                    if behind:
                        weights(g - 2, u, o, False)
                    if ahead:
                        make_mask(g, 3, more)
                        between()
                        take_keys(g, 0, o)
                        between()
                        take_keys(g, 1, o)
                        between()
                        decode(g, u, o)
                        between()
                    if behind:
                        finish(b, g - 2, u, o)
                    if ahead:
                        dve.wait_ge(pensT_ready, g + 1)
                        nc.vector.tensor_reduce(need[:, u:u + 1], pensT, AX, ALU.min).then_inc(need_ready, 1)
                    if not behind and u:
                        node_scores()

            o = Order(dve, vloop)
            for n in range(NODE_STEPS[0][0]):
                node_step(n)
            emit(0, True, False, o)
            first = o.n
            emit(1, True, True, o)
            peeled, per_body = o.n, o.n - first
            with dve.Fori(2, NB) as b:
                o = Order(dve, vloop, peeled + (b - 2) * per_body)
                emit(b, True, True, o)
            assert o.n == per_body

            dve.wait_ge(flagT_ready, 1)
            nc.vector.tensor_reduce(f_flag_c[:, :], small[0:NT, 384:384 + P], AX, ALU.max).then_inc(flag_col_ready, 1)
            dve.wait_ge(flag_row_ready, 1)
            flag_row = small[0:1, 0:NT]
            v.then(nc.vector.tensor_tensor(f_keys[:, :], flag_row, f_order[:, :], ALU.mult))
            v.then(nc.vector.tensor_reduce(f_counted[:, :], flag_row, AX, ALU.add))
            v.settle()
            for k in range(0, NT, 8):
                v.then(nc.vector.max(f_sorted[:, k:k + 8], f_keys[:, :]))
                v.settle()
                if k + 8 < NT:
                    v.then(nc.vector.match_replace(out=f_keys[:, :], in_to_replace=f_sorted[:, k:k + 8],
                                                   in_values=f_keys[:, :], imm_value=0.0))
                    v.settle()
            v.then(nc.vector.tensor_scalar(f_list[:, 0:NT], f_sorted[:, :], -1.0, float(NT), ALU.mult, ALU.add))
            v.settle()
            nc.vector.tensor_copy(f_count[:, :], f_counted[:, :]).then_inc(flags_ready, 1)

            o = Order(dve, vloop, peeled + (NB - 2) * per_body)

            neg_m, z_max, m_slope, m_one, signs, deg, z_sum, inv, gain, least, scale = (
                f_row[:, c:c + 1] for c in range(11))

            def f_scores(j):
                t = dve.value_load(f_list[0:1, bass.ds(j, 1)], min_val=0, max_val=NT - 1)
                o = Order(dve, fchain, j * F_CHAIN)
                for c in range(FQ):
                    dve.wait_ge(f_pen_ready, j * FQ + c + 1)
                    stand_apart(dve)
                    nc.vector.tensor_tensor_reduce(out=f_e[:, c, :], in0=f_d[:, c, :], in1=f_e[:, c, :], scale=1.0,
                                                   scalar=-3e38, op0=ALU.subtract, op1=ALU.max,
                                                   accum_out=f_max[:, c:c + 1]).then_inc(f_d_ready, 1)
                dve.wait_ge(f_d_ready, (j + 1) * FQ)
                o.then(nc.vector.tensor_reduce(z_max, f_max[:, :], AX, ALU.max))
                o.settle()
                o.then(nc.vector.tensor_scalar(m_slope, z_max, s_all[:, bass.ds(t, 1)], -SLOPE, ALU.add, ALU.mult))
                o.then(nc.vector.tensor_scalar(m_one, z_max, s_all[:, bass.ds(t, 1)], -1.0, ALU.add, ALU.mult))
                o.settle()
                nc.vector.tensor_tensor(neg_m, m_slope, m_one, ALU.min).then_inc(f_m_ready, 1)
                for c in range(FQ):
                    dve.wait_ge(f_z_ready, j * FQ + c + 1)
                    nc.vector.scalar_tensor_tensor(f_e[:, c, :], f_z[:, c, :], SLOPE, f_z[:, c, :],
                                                   ALU.mult, ALU.max).then_inc(f_e_ready, 1)
                return o

            def f_weights(j, o):
                dve.wait_ge(f_q_ready, (j + 1) * FQ)
                o.then(nc.vector.tensor_reduce(z_sum, f_sum[:, :], AX, ALU.add))
                o.settle()
                nc.vector.tensor_scalar(least, z_sum, THR, None, ALU.mult).then_inc(f_least_ready, 1)
                dve.wait_ge(f_least_ready, j + 1)
                for c in range(FQ):
                    nc.vector.scalar_tensor_tensor(f_e[:, c, :], f_e[:, c, :], least, f_e[:, c, :],
                                                   ALU.is_ge, ALU.mult).then_inc(f_w_ready, 1)

            def f_finish(j, o):
                t = dve.value_load(f_list[0:1, bass.ds(j, 1)], min_val=0, max_val=NT - 1)
                dve.wait_ge(f_signs_ready, (j + 1) * FQ)
                o.then(nc.vector.tensor_reduce(signs, f_signs[:, :], AX, ALU.add))
                o.then(nc.vector.reciprocal(inv, z_sum))
                o.settle()
                o.then(nc.vector.tensor_scalar(deg, signs, float(N), 0.5, ALU.add, ALU.mult))
                o.settle()
                o.then(nc.vector.scalar_tensor_tensor(gain, inv, THR, deg, ALU.is_gt, ALU.mult))
                o.settle()
                nc.vector.tensor_tensor(scale, gain, inv, ALU.mult).then_inc(f_scale_ready, 1)
                assert o.n == F_CHAIN, o.n
                dve.wait_ge(f_scale_ready, j + 1)
                dve.wait_ge(f_T_used, (j + 1) * F_CHUNKS)
                nc.vector.scalar_tensor_tensor(f_y[:, :], agg[0][:, 0:D], scale,
                                               f_h[:, bass.ds(t, 1), 0:D].rearrange("p t d -> p (t d)"),
                                               ALU.mult, ALU.add).then_inc(f_y_ready, 1)
                dve.wait_ge(f_expy_ready, j + 1)
                dve.wait_ge(f_x_in, 16 * (j + 1))
                nc.vector.scalar_tensor_tensor(elu1[:, 0, :], f_y[:, :], 0.0, expy[:, 0, :],
                                               ALU.max, ALU.add).then_inc(f_out_ready, 1)
                dve.wait_ge(f_out_ready, 2 * j + 1)
                nc.vector.scalar_tensor_tensor(f_out[:, :], elu1[:, 0, :], -1.0, f_x[:, :],
                                               ALU.add, ALU.add).then_inc(f_out_ready, 1)
                dve.wait_ge(f_stored, 16 * (j + 1))
                stand_apart(dve)

            def f_tile(j):
                o = f_scores(j)
                f_weights(j, o)
                f_finish(j, o)

            scores(NB, NG - 2, 0, o)
            weights(NG - 2, 0, o, False)
            finish(NB, NG - 2, 0, o)
            dve.wait_ge(flags_ready, 1)
            count = dve.value_load(f_count[0:1, 0:1], min_val=0, max_val=NT)
            with dve.If(count > 0):
                dve.wait_ge(f_d_in, 16)
                fo = f_scores(0)
            scores(NB, NG - 1, 1, o)
            weights(NG - 1, 1, o, False)
            with dve.If(count > 0):
                f_weights(0, fo)
            finish(NB, NG - 1, 1, o)
            with dve.If(count > 0):
                dve.wait_ge(f_h_in, 16)
                f_finish(0, fo)
            for_other_flagged(dve, count, f_tile)

        @block.tensor
        def _(pe):
            pe.wait_ge(consts, CONSTS)
            pe.wait_ge(w_in, 48)
            nc.tensor.transpose(misc[:, 0:P], w_sb[:, :], ident[:, :]).then_inc(wT_ps_ready, 1)
            pe.wait_ge(wT_ready, 1)
            nc.tensor.matmul(misc[:, P:P + 3], wT[:, :], a_sb[:, :], start=True, stop=True).then_inc(wa_ps_ready, 1)
            pe.wait_ge(wa_ready, 1)

            def transposes(n):
                pe.wait_ge(x_loaded[(n * QT) // XT], 16)
                if n:
                    pe.wait_ge(xT_ready, n)
                for i in range(QT):
                    last = nc.tensor.transpose(xT_ps[:, i * P:(i + 1) * P], xs[:, QT * n + i, :], ident[:, :])
                last.then_inc(xT_ps_ready, 1)

            def node_step(n):
                pe.wait_ge(xT_ready, n + 1)
                if n:
                    pe.wait_ge(relT_ready, n)
                    pe.wait_ge(sqT_ready, n)
                nc.tensor.matmul(xc_ps[:, :], center[:, :], xT[:, :], start=True, stop=True).then_inc(xc_ready, 1)
                if n + 1 < NQ:
                    transposes(n + 1)
                pe.wait_ge(relT_ready, n + 1)
                pe.wait_ge(sqT_ready, n + 1)
                if n:
                    pe.wait_ge(h_ready, n)
                for i in range(QT):
                    cols = slice(i * P, (i + 1) * P)
                    t = QT * n + i
                    nc.tensor.matmul(var_ps[:, t:t + 1], sqT[:, cols], mean_w[:, :], start=True, stop=True)
                    nc.tensor.matmul(ds_ps[:, t, :], relT[:, cols], wa[:, :], start=True, stop=True)
                    last = nc.tensor.matmul(h_ps[:, i * D:(i + 1) * D], relT[:, cols], w_sb[:, :], start=True, stop=True)
                last.then_inc(h_ps_ready, 1)

            transposes(0)
            for n in range(NODE_STEPS[0][0]):
                node_step(n)

            def pack(g, r, more):
                i, half = divmod(r, 2)
                wait_mask(pe, g, r)
                if half == 0 and more:
                    pe.wait_ge(keys_taken, GT * (g - 1) + i + 1)
                for bk in range(2):
                    bank = packed[2 * i + bk][:, :].rearrange("p (a c) -> p a c", a=2)

                    def of_bank(cells):
                        return cells.rearrange("p (a b c) -> p b a c", b=2, c=SPLIT)[:, bk, :, :]

                    if half == 0:
                        nc.tensor.matmul(bank, cell_w[0:2, :], of_bank(cell_no[0:2, :]), start=True, stop=False)
                    for k in range(PACK // 2):
                        last = nc.tensor.matmul(bank, pack_w[:, half * (PACK // 2) + k, :],
                                                of_bank(mask_ring[:, r, k * CELLS:(k + 1) * CELLS]), start=False,
                                                stop=(half == 1 and k == PACK // 2 - 1))
                last.then_inc(packed_ready, 1)

            def weigh(b, g, u, first):
                for i in range(GT):
                    acc = agg[u][:, i * D:(i + 1) * D]
                    left = pe.value_load(need[i:i + 1, u:u + 1], min_val=0, max_val=SLOTS * PEN)
                    base = (GT * g + i) * SLOTS
                    if i == 0:
                        pe.wait_ge(xh_in[u], 32 * b)
                        if not first:
                            pe.wait_ge(out_ready, g - 1)
                        pe.wait_ge(gathered[u], 16 * GT * SLOTS * b)

                    def rows(k0, k1):
                        for k in range(k0, k1):
                            pe.wait_ge(diag_ready, base + k + 1)
                            nc.tensor.matmul(acc, diag[:, k % DIAG, :], G[:, u, i, k, 0:D], start=(k == 0),
                                             stop=False).then_inc(diag_used, 1)

                    rows(0, DIAG)
                    for k0, k1 in DIAG_STEPS:
                        with pe.If(left < (SLOTS - k0) * PEN):
                            rows(k0, k1)
                        with pe.Else():
                            pe.drain().then_inc(diag_used, k1 - k0)
                    last = nc.tensor.matmul(acc, ident[:, :], h_in[:, u, i, 0:D], start=False, stop=True)
                last.then_inc(agg_ready, 1)

            def emit(b, ahead, behind, first=False):
                for u in range(2):
                    g = 2 * b + u
                    nodes = [] if behind else list(NODE_STEPS[u])
                    if ahead:
                        for r in range(4):
                            pack(g, r, behind or u)
                            for _ in range(1 + r % 2):
                                if nodes:
                                    if u:
                                        pe.wait_ge(need_ready, u)
                                    node_step(nodes.pop(0))
                    if behind:
                        weigh(b, g - 2, u, first)
                    if ahead:
                        pe.wait_ge(pens_ready, g + 1)
                        if behind or u:
                            pe.wait_ge(need_ready, g)
                        if not behind and u:
                            pe.wait_ge(std_ready, NX)
                        nc.tensor.transpose(pensT, pens[:, :], ident[:, :]).then_inc(pensT_ready, 1)
                    if not behind and u:
                        pe.wait_ge(h_ready, NQ)
                        pe.wait_ge(d_ok_ready, 1)
                        nc.tensor.transpose(misc[0:NT, 0:P], d_ok[:, :], ident[:, :]).then_inc(dT_ps_ready, 1)

            emit(0, True, False)
            emit(1, True, True, True)
            with pe.Fori(2, NB) as b:
                emit(b, True, True)
            pe.wait_ge(need_ready, NG)
            nc.tensor.transpose(small[0:NT, 384:384 + P], flag_all[:, :], ident[:, :]).then_inc(flagT_ready, 1)
            pe.wait_ge(flag_col_ready, 1)
            nc.tensor.transpose(small[0:1, 0:NT], f_flag_c[:, :], ident[0:NT, 0:NT]).then_inc(flag_row_ready, 1)
            emit(NB, False, True)

            pe.wait_ge(flags_ready, 1)
            pe.wait_ge(f_h_in, 16)
            pe.wait_ge(out_ready, NG - 1)

            def f_tile(j):
                def f_transposes(c):
                    if c >= 2:
                        pe.wait_ge(f_T_ready, j * F_CHUNKS + c - 1)
                    pe.wait_ge(f_w_ready, j * FQ + c // 4 + 1)
                    for i in range(QT):
                        c0 = (c % 4 * QT + i) * P
                        last = nc.tensor.transpose(banks[c % 2][:, i * P:(i + 1) * P],
                                                   f_e[:, c // 4, c0:c0 + P], ident[:, :])
                    last.then_inc(f_T_ps_ready, 1)

                f_transposes(0)
                for c in range(F_CHUNKS):
                    if c + 1 < F_CHUNKS:
                        f_transposes(c + 1)
                    pe.wait_ge(f_T_ready, j * F_CHUNKS + c + 1)
                    for i in range(QT):
                        last = nc.tensor.matmul(agg[0][:, 0:D], f_T[:, c % 2, i * P:(i + 1) * P],
                                                f_h[:, QT * c + i, 0:D], start=(c == 0 and i == 0),
                                                stop=(c == F_CHUNKS - 1 and i == QT - 1))
                    last.then_inc(f_T_used, 1)
                pe.wait_ge(f_y_ready, j + 1)
                stand_apart(pe)

            count = pe.value_load(f_count[0:1, 0:1], min_val=0, max_val=NT)
            with pe.If(count > 0):
                f_tile(0)
            for_other_flagged(pe, count, f_tile)


_INS = ["x", "adj", "L0_gnn_W", "L0_gnn_a"]
_OUTS = [((8192, 128), "float32")]


def kernel(**inputs):
    import numpy as _np
    import concourse.bacc as _bacc
    from concourse import mybir as _mybir
    from concourse.bass_utils import run_bass_kernel_spmd as _run

    nc = _bacc.Bacc("TRN2", target_bir_lowering=False, num_devices=1)
    arrays, args = {}, []
    for name in _INS:
        a = _np.ascontiguousarray(inputs[name])
        arrays[f"in_{name}_dram"] = a
        args.append(nc.dram_tensor(f"in_{name}_dram", a.shape, _mybir.dt.from_np(a.dtype), kind="ExternalInput").ap())
    for i, (shape, dtype) in enumerate(_OUTS):
        dt = _mybir.dt.from_np(_np.dtype(dtype))
        args.append(nc.dram_tensor(f"out_{i}_dram", shape, dt, kind="ExternalOutput").ap())
    gat_kernel(nc, *args)
    r = _run(nc, [arrays], core_ids=[0])
    return r.results[0]["out_0_dram"]
```

```python
import concourse.bass as bass
from concourse import mybir
from contextlib import ExitStack

FP32 = mybir.dt.float32
BF16 = mybir.dt.bfloat16
I32 = mybir.dt.int32
ALU = mybir.AluOpType
ACT = mybir.ActivationFunctionType
AX = mybir.AxisListType.X

P = 128
LN_EPS = 1e-5
SLOPE = 0.2
THR = 1e-4
BIG = 1e30
F_BIG = 4e28
VALID_ABOVE = -1e28


def gat_kernel(nc, x, adj, w, a, out):
    N, D = x.shape
    NT = N // P
    HALF = N // 2
    GT = 2
    NG = NT // GT
    NB = NG // 2
    CELLS = 1024
    PACK = N // CELLS
    BANK = 512
    SPLIT = 256
    RUN = 16
    SEGS = 4
    KEYS = 2 * SEGS * 8
    SLOTS = 32
    ROW = D + 1
    QT = 4
    NQ = NT // QT
    PT = 2
    NX = 4
    XT = NT // NX
    WIDE = D + 3
    DIAG = 8
    EXP_OFF = (127 + 10) * CELLS
    PEN = 1 << 20
    EXP_MASK = 0x7F800000

    table = nc.dram_tensor("table", (N, ROW), FP32, kind="Internal").ap()
    d_line = nc.dram_tensor("d_line", (N // P, P), FP32, kind="Internal").ap()

    x_t = x.rearrange("(t p) d -> p t d", p=P)
    out_t = out.rearrange("(t p) d -> p t d", p=P)
    table_t = table.rearrange("(t p) r -> p t r", p=P)
    x_g = x.rearrange("(i g p) d -> p i g d", p=P, g=NG)
    out_g = out.rearrange("(i g p) d -> p i g d", p=P, g=NG)
    table_g = table.rearrange("(i g p) r -> p i g r", p=P, g=NG)
    adj_t = adj.rearrange("(t p) (h c) -> p t h c", p=P, h=2)
    adj_q = adj.rearrange("(t p) (q c) -> p t q c", p=P, q=4)

    ctx = ExitStack()
    with ctx:
        def sb(name, shape, dt):
            return ctx.enter_context(nc.sbuf_tensor(name, shape, dt))

        def pb(name, shape, dt=FP32):
            return ctx.enter_context(nc.psum_tensor(name, shape, dt))

        def sem(name):
            return ctx.enter_context(nc.semaphore(name))

        adj_ring = sb("adj_ring", [P, 4, HALF], I32)
        mask_ring = sb("mask_ring", [P, 4, HALF], BF16)
        gbuf = sb("gbuf", [P, NT * (D + WIDE)], FP32)
        assert NT * (D + WIDE) >= 2 * GT * SLOTS * ROW
        G = gbuf[:, 0:2 * GT * SLOTS * ROW].rearrange("p (b i k r) -> p b i k r", b=2, i=GT, k=SLOTS)
        ident = sb("ident", [P, P], FP32)
        pack_w = sb("pack_w", [P, PACK, P], BF16)
        cell_no = sb("cell_no", [2, CELLS], BF16)
        cell_w = sb("cell_w", [2, P], BF16)
        s_all = sb("s_all", [P, NT], FP32)
        flag_all = sb("flag_all", [P, NT], FP32)
        V = sb("V", [P, GT, 2, KEYS], FP32)
        kint = sb("kint", [P, GT, KEYS], I32)
        cell = sb("cell", [P, GT, KEYS], I32)
        hib = sb("hib", [P, GT, 2, KEYS], I32)
        expo = sb("expo", [P, GT, 2, KEYS], I32)
        cand = sb("cand", [P, GT, 2, KEYS], FP32)
        rest = sb("rest", [P, GT, KEYS], FP32)
        mx = sb("mx", [P, 4, GT], FP32)
        top = sb("top", [P, GT, SLOTS], FP32)
        pen = sb("pen", [P, 2, GT, SLOTS], FP32)
        idx = sb("idx", [P, 2, GT, SLOTS], I32)
        pen_sum = sb("pen_sum", [P, GT], FP32)
        pens = sb("pens", [P, GT], FP32)
        least = sb("least", [GT, 2], FP32)
        need = sb("need", [GT, 2], I32)
        xm = sb("xm", [P, GT, SLOTS], FP32)
        e = sb("e", [P, GT, SLOTS], FP32)
        em = sb("em", [P, GT, SLOTS], FP32)
        q = sb("q", [P, GT, SLOTS], FP32)
        att = sb("att", [P, GT, SLOTS], FP32)
        keep = sb("keep", [P, GT, SLOTS], FP32)
        valid = sb("valid", [P, GT, SLOTS], FP32)
        wts = sb("wts", [P, GT, SLOTS], FP32)
        r_max = sb("r_max", [P, GT], FP32)
        r_sum = sb("r_sum", [P, GT], FP32)
        r_inv = sb("r_inv", [P, GT], FP32)
        r_deg = sb("r_deg", [P, GT], FP32)
        r_gain = sb("r_gain", [P, GT], FP32)
        diag = sb("diag", [P, DIAG, P], FP32)
        x_in = sb("x_in", [P, 2, GT, D], FP32)
        h_in = sb("h_in", [P, 2, GT, ROW], FP32)
        negy = sb("negy", [P, GT, D], FP32)
        expy = sb("expy", [P, GT, D], FP32)
        elu1 = sb("elu1", [P, GT, D], FP32)
        out_sb = sb("out_sb", [P, 2, GT, D], FP32)

        banks = [pb(f"bank{i}", [P, BANK]) for i in range(8)]
        packed = banks[0:4]
        agg = banks[4:6]
        small = banks[6]
        pensT = small[0:GT, 256:256 + P]

        xs = gbuf[:, 0:NT * D].rearrange("p (t d) -> p t d", d=D)
        ts = gbuf[:, NT * D:NT * (D + WIDE)].rearrange("p (t r) -> p t r", r=WIDE)
        w_ext = sb("w_ext", [P, WIDE], FP32)
        a_sb = sb("a_sb", [P, 3], FP32)
        wT = sb("wT", [P, P], FP32)
        sums = sb("sums", [P, NT], FP32)
        neg_mean = sb("neg_mean", [P, NT], FP32)
        sq = sb("sq", [P, XT, D], FP32)
        sq_sums = sb("sq_sums", [P, NT], FP32)
        std = sb("std", [P, NT], FP32)
        rstd = sb("rstd", [P, NT], FP32)
        hz = sb("hz", [P, NT], FP32)
        d_ok = sb("d_ok", [P, NT], FP32)
        dT = sb("dT", [NT, P], FP32)
        eps = sb("eps", [P, 1], FP32)
        relT = sb("relT", [P, 2, QT * P], FP32)
        xT_ps = [banks[4], banks[6]]
        h_ps = [banks[5], banks[7], *packed]
        HB = len(h_ps)
        misc = banks[7]

        FQ = 4
        f_adj = adj_ring[:, 0:2, :].rearrange("p h c -> p (h c)").rearrange("p (q c) -> p q c", q=FQ)
        f_z = f_adj.bitcast(FP32)
        f_e = adj_ring[:, 2:4, :].rearrange("p h c -> p (h c)").bitcast(FP32).rearrange("p (q c) -> p q c", q=FQ)
        f_d = mask_ring[:, :, :].rearrange("p r c -> p (r c)").bitcast(FP32).rearrange("p (q c) -> p q c", q=FQ)
        f_h = G[:, 0, :, :, :].rearrange("p i k r -> p (i k) r")
        f_rest = GT * SLOTS * ROW
        f_T = gbuf[:, f_rest:f_rest + 2 * BANK].rearrange("p (b c) -> p b c", b=2)
        f_sign = gbuf[:, f_rest + 2 * BANK:f_rest + 2 * BANK + N // FQ]
        f_flag_c = sb("f_flag_c", [NT, 1], FP32)
        f_order = sb("f_order", [1, NT], FP32)
        f_keys = sb("f_keys", [1, NT], FP32)
        f_sorted = sb("f_sorted", [1, NT], FP32)
        f_list = sb("f_list", [1, NT + 1], I32)
        f_counted = sb("f_counted", [1, 1], FP32)
        f_count = sb("f_count", [1, 1], I32)
        f_x = sb("f_x", [P, D], FP32)
        f_y = sb("f_y", [P, D], FP32)
        f_out = sb("f_out", [P, D], FP32)
        f_far = sb("f_far", [P, 1], FP32)
        f_big = sb("f_big", [P, 1], FP32)
        f_max = sb("f_max", [P, FQ], FP32)
        f_sum = sb("f_sum", [P, FQ], FP32)
        f_signs = sb("f_signs", [P, FQ], FP32)
        f_row = sb("f_row", [P, 11], FP32)

        ident0 = sem("ident0")
        consts = sem("consts")
        w_in = sem("w_in")
        x_loaded = [sem(f"x_loaded{c}") for c in range(NX)]
        vchain = sem("vchain")
        vloop = sem("vloop")
        mean_ready = sem("mean_ready")
        xc_ready = sem("xc_ready")
        sq_ready = sem("sq_ready")
        var_ready = sem("var_ready")
        std_ready = sem("std_ready")
        rstd_ready = sem("rstd_ready")
        wT_ps_ready = sem("wT_ps_ready")
        wT_ready = sem("wT_ready")
        wa_ps_ready = sem("wa_ps_ready")
        wa_ready = sem("wa_ready")
        xT_ps_ready = sem("xT_ps_ready")
        relT_ready = sem("relT_ready")
        h_ps_ready = sem("h_ps_ready")
        h_ready = sem("h_ready")
        d_ok_ready = sem("d_ok_ready")
        rows_ready = sem("rows_ready")
        dT_ps_ready = sem("dT_ps_ready")
        dT_ready = sem("dT_ready")
        table_stored = sem("table_stored")
        d_stored = sem("d_stored")

        adj_in = [sem(f"adj_in{r}") for r in range(4)]
        wait_passed = sem("wait_passed")
        mask_ready = sem("mask_ready")
        mask0_ready = sem("mask0_ready")
        relu0_ready = sem("relu0_ready")
        packed_ready = sem("packed_ready")
        keys_taken = sem("keys_taken")
        idx_ready = sem("idx_ready")
        pens_ready = sem("pens_ready")
        pensT_ready = sem("pensT_ready")
        need_ready = sem("need_ready")
        gathered = [sem(f"gathered{u}") for u in range(2)]
        em_ready = sem("em_ready")
        q_ready = sem("q_ready")
        wts_ready = sem("wts_ready")
        diag_ready = sem("diag_ready")
        diag_used = sem("diag_used")
        xh_in = [sem(f"xh_in{u}") for u in range(2)]
        agg_ready = sem("agg_ready")
        negy_ready = sem("negy_ready")
        expy_ready = sem("expy_ready")
        out_ready = sem("out_ready")
        out_stored = [sem(f"out_stored{u}") for u in range(2)]

        flagT_ready = sem("flagT_ready")
        flag_col_ready = sem("flag_col_ready")
        flag_row_ready = sem("flag_row_ready")
        flags_ready = sem("flags_ready")
        list_ready = sem("list_ready")
        f_d_in = sem("f_d_in")
        f_h_in = sem("f_h_in")
        f_in = [sem(f"f_in{c}") for c in range(FQ)]
        f_x_in = sem("f_x_in")
        fchain = sem("fchain")
        f_pen_ready = sem("f_pen_ready")
        f_d_ready = sem("f_d_ready")
        f_z_ready = sem("f_z_ready")
        f_signs_ready = sem("f_signs_ready")
        f_m_ready = sem("f_m_ready")
        f_e_ready = sem("f_e_ready")
        f_y_ready = sem("f_y_ready")
        f_least_ready = sem("f_least_ready")
        f_scale_ready = sem("f_scale_ready")
        f_q_ready = sem("f_q_ready")
        f_w_ready = sem("f_w_ready")
        f_T_ps_ready = sem("f_T_ps_ready")
        f_T_ready = [sem(f"f_T_ready{c}") for c in range(2)]
        f_T_used = sem("f_T_used")
        f_negy_ready = sem("f_negy_ready")
        f_expy_ready = sem("f_expy_ready")
        f_out_ready = sem("f_out_ready")
        f_stored = sem("f_stored")

        GATHER_STEPS = [(4, 6), (6, 7), (7, 8), (8, 9), (9, 10), (10, 11), (11, 12), (12, 14), (14, 16),
                        (16, 20), (20, 24), (24, 28), (28, SLOTS)]
        DIAG_STEPS = [(DIAG, 12), (12, 16), (16, SLOTS)]

        CONSTS = PACK + 8
        F_CHUNKS = N // BANK
        FV = 3
        F_CHAIN = FV + 8
        F_BLOCK = 9
        assert (NT - 1) % F_BLOCK == 0

        def wait_mask(eng, g, r):
            if r == 0:
                eng.wait_ge(mask0_ready, g + 1)
            else:
                eng.wait_ge(mask_ready, 3 * g + r)

        def of_group(columns, g):
            return columns[:, :].rearrange("p (i g) -> p i g", g=NG)[:, :, bass.ds(g, 1)].rearrange("p i g -> p (i g)")

        class Order:

            def __init__(self, eng, s, base=0):
                self.eng, self.s, self.base, self.n = eng, s, base, 0

            def then(self, ins):
                ins.then_inc(self.s, 1)
                self.n += 1

            def settle(self, apart=False):
                self.eng.wait_ge(self.s, self.base + self.n)
                if apart:
                    stand_apart(self.eng)

        def stand_apart(eng):
            eng.sem_inc(wait_passed, 1)

        def for_other_flagged(eng, count, work):
            with eng.If(count > 1):
                eng.wait_ge(list_ready, NT // 8)
                with eng.Fori(0, (NT - 1) // F_BLOCK) as jb:
                    with eng.If(count > jb * F_BLOCK + 1):
                        with eng.Fori(0, F_BLOCK) as ji:
                            with eng.If(count > jb * F_BLOCK + ji + 1):
                                work(jb * F_BLOCK + ji + 1)

        def as_needed(eng, left, steps, work, skip):
            k0, k1 = steps[0]
            with eng.If(left < (SLOTS - k0) * PEN):
                work(k0, k1)
                if steps[1:]:
                    as_needed(eng, left, steps[1:], work, skip)
            with eng.Else():
                skip(SLOTS - k0)

        block = ctx.enter_context(nc.Block())

        @block.sync
        def _(sp):
            def x_load(c):
                sp.dma_start(xs[:, c * XT:(c + 1) * XT, :], x_t[:, c * XT:(c + 1) * XT, :]).then_inc(x_loaded[c], 16)

            x_load(0)
            sp.dma_start(w_ext[:, 0:D], w[:, :]).then_inc(w_in, 16)
            for c in range(2):
                sp.dma_start(a_sb[:, c:c + 1], a[(1 - c) * D:(2 - c) * D, :]).then_inc(w_in, 16)
            for c in range(1, NX):
                x_load(c)
            for r in range(4):
                sp.dma_start(adj_ring[:, r, :], adj_t[:, NG * (r // 2), r % 2, :]).then_inc(adj_in[r], 16)

            def adj_loads(g, last):
                if last:
                    return
                for r in range(4):
                    wait_mask(sp, g, r)
                    sp.dma_start(adj_ring[:, r, :], adj_t[:, g + 1 + NG * (r // 2), r % 2, :]).then_inc(adj_in[r], 16)

            def body(b, ahead, behind, final):
                for u in range(2):
                    g = 2 * b + u
                    if ahead:
                        adj_loads(g, final and u == 1)
                    if isinstance(g, int) and g == 1:
                        sp.wait_ge(dT_ready, 1)
                        sp.dma_start(d_line, dT[:, :]).then_inc(d_stored, 16)
                        sp.wait_ge(table_stored, 16 * NX)
                    if final and u == 1:
                        sp.wait_ge(packed_ready, 4 * NG)
                        sp.wait_ge(d_stored, 16)
                        sp.dma_start(mask_ring[:, :, :].rearrange("p r c -> p (r c)").bitcast(FP32),
                                     d_line.rearrange("(o t) p -> o (t p)", o=1).to_broadcast([P, N])).then_inc(f_d_in, 16)
                    if behind:
                        sp.wait_ge(out_ready, g - 2 + 1)
                        sp.dma_start(out_g[:, :, g - 2, :], out_sb[:, u, :, :]).then_inc(out_stored[u], 16)
                    own = [(g, u)] if ahead else []
                    if not behind:
                        own = [(0, 0), (1, 1)] if u else []
                    for gg, uu in own:
                        sp.dma_start(x_in[:, uu, :, :], x_g[:, :, gg, :]).then_inc(xh_in[uu], 16)
                        sp.dma_start(h_in[:, uu, :, :], table_g[:, :, gg, :]).then_inc(xh_in[uu], 16)

            for c in range(NX):
                cs = slice(c * XT, (c + 1) * XT)
                sp.wait_ge(rows_ready, c + 1)
                sp.dma_start(table_t[:, cs, :], ts[:, cs, 0:ROW]).then_inc(table_stored, 16)

            def f_tile(j):
                t = sp.value_load(f_list[0:1, bass.ds(j, 1)], min_val=0, max_val=NT - 1)
                sp.dma_start(f_x[:, :], x_t[:, t, :]).then_inc(f_x_in, 16)
                with sp.If(count > j + 1):
                    f_loads(j + 1)
                sp.wait_ge(f_out_ready, 2 * (j + 1))
                sp.dma_start(out_t[:, t, :], f_out[:, :]).then_inc(f_stored, 16)
                sp.wait_ge(f_stored, 16 * (j + 1))
                stand_apart(sp)

            body(0, True, False, False)
            with sp.Fori(1, NB - 1) as b:
                body(b, True, True, False)
            body(NB - 1, True, True, True)

            sp.wait_ge(flags_ready, 1)
            sp.wait_ge(list_ready, 1)
            count = sp.value_load(f_count[0:1, 0:1], min_val=0, max_val=NT)

            def f_loads(j):
                t = sp.value_load(f_list[0:1, bass.ds(j, 1)], min_val=0, max_val=NT - 1)
                for c in range(FQ):
                    if not (isinstance(j, int) and j == 0):
                        sp.wait_ge(f_signs_ready, (j - 1) * FQ + c + 1)
                        sp.wait_ge(f_e_ready, (j - 1) * FQ + c + 1)
                    sp.dma_start(f_adj[:, c, :], adj_q[:, t, c, :]).then_inc(f_in[c], 16)

            with sp.If(count > 0):
                f_loads(0)
            sp.wait_ge(agg_ready, NG - 1)
            sp.dma_start(f_h, table_t).then_inc(f_h_in, 16)
            body(NB, False, True, False)
            for u in range(2):
                sp.wait_ge(out_stored[u], 16 * NB)

            with sp.If(count > 0):
                f_tile(0)
            for_other_flagged(sp, count, f_tile)
            sp.wait_ge(f_d_in, 16)
            sp.wait_ge(f_h_in, 16)

        @block.gpsimd
        def _(pool):
            pool.memset(ident[:, :], 0.0).then_inc(ident0, 1)
            pool.memset(pack_w[:, :, :], 0.0).then_inc(ident0, 1)
            pool.memset(eps[:, :], LN_EPS).then_inc(consts, 1)
            pool.memset(a_sb[:, 2:3], 1.0).then_inc(consts, 1)
            pool.iota(f_order[:, :], pattern=[[-1, NT]], base=NT, channel_multiplier=0,
                      allow_small_or_imprecise_dtypes=True).then_inc(consts, 1)
            pool.memset(f_far[:, :], -VALID_ABOVE).then_inc(consts, 1)
            pool.memset(f_big[:, :], F_BIG).then_inc(consts, 1)
            pool.wait_ge(ident0, 2)
            pool.affine_select(out=ident[:, :], in_=ident[:, :], compare_op=ALU.not_equal, fill=1.0, base=0,
                               pattern=[[-1, P]], channel_multiplier=1).then_inc(consts, 1)
            for k in range(PACK):
                pool.affine_select(out=pack_w[:, k, :], in_=pack_w[:, k, :], compare_op=ALU.not_equal,
                                   fill=float(CELLS << k), base=0, pattern=[[-1, P]],
                                   channel_multiplier=1).then_inc(consts, 1)
            pool.iota(cell_no[0:2, :].rearrange("p (a c) -> p a c", c=256), pattern=[[0, CELLS // 256], [1, 256]],
                      base=0, channel_multiplier=0, allow_small_or_imprecise_dtypes=True).then_inc(ident0, 1)
            pool.memset(cell_w[0:2, :], 1.0).then_inc(ident0, 1)
            pool.wait_ge(ident0, 4)
            pool.iota(cell_no[0:1, :].rearrange("p (a c) -> p a c", c=256), pattern=[[1, CELLS // 256], [0, 256]],
                      base=0, channel_multiplier=0, allow_small_or_imprecise_dtypes=True).then_inc(consts, 1)
            pool.memset(cell_w[0:1, :], 256.0).then_inc(consts, 1)

            for c in range(NX):
                cs = slice(c * XT, (c + 1) * XT)
                pool.wait_ge(mean_ready, c + 1)
                pool.tensor_tensor(xs[:, cs, :], xs[:, cs, :],
                                   neg_mean[:, cs].unsqueeze(2).to_broadcast([P, XT, D]), ALU.add).then_inc(xc_ready, 1)
            pool.wait_ge(table_stored, 16 * NX)

            def emit(b, ahead, behind):
                if not ahead:
                    return
                for u in range(2):
                    g = 2 * b + u
                    pool.wait_ge(need_ready, g + 1)
                    pool.wait_ge(idx_ready, g + 1)
                    if behind:
                        pool.wait_ge(agg_ready, g - 1)
                    stand_apart(pool)
                    for i in range(GT):
                        left = pool.value_load(need[i:i + 1, u:u + 1], min_val=0, max_val=SLOTS * PEN)

                        def gather(k):
                            pool.indirect_dma_start(
                                out=G[:, u, i, k, :], out_offset=None, in_=table[:, :],
                                in_offset=bass.IndirectOffsetOnAxis(ap=idx[:, u, i, k:k + 1], axis=0),
                                bounds_check=N - 1, oob_is_err=False).then_inc(gathered[u], 16)

                        for k in range(GATHER_STEPS[0][0]):
                            gather(k)
                        as_needed(pool, left, GATHER_STEPS, lambda k0, k1: [gather(k) for k in range(k0, k1)],
                                  lambda slots: pool.inc_swdge_sem([gathered[u]], [16 * slots]))

            emit(0, True, False)
            with pool.Fori(1, NB) as b:
                emit(b, True, True)
        @block.scalar
        def _(act):
            act.wait_ge(consts, CONSTS)

            def squares(c):
                act.wait_ge(xc_ready, c + 1)
                if c:
                    act.wait_ge(var_ready, c)
                nc.scalar.activation(sq[:, :, :], xs[:, c * XT:(c + 1) * XT, :], ACT.Square).then_inc(sq_ready, 1)

            def deviations(c):
                act.wait_ge(var_ready, c + 1)
                nc.scalar.activation(std[:, c * XT:(c + 1) * XT], sq_sums[:, c * XT:(c + 1) * XT], ACT.Sqrt,
                                     scale=1.0 / D, bias=eps[:, 0:1]).then_inc(std_ready, 1)

            def relus(n0, n1):
                for n in range(n0, n1):
                    act.wait_ge(xT_ps_ready, n + 1)
                    if n >= 2:
                        act.wait_ge(h_ps_ready, QT // PT * (n - 1))
                    nc.scalar.activation(relT[:, n % 2, :], xT_ps[n % 2][:, :], ACT.Relu).then_inc(relT_ready, 1)

            def make_mask0(g):
                act.wait_ge(adj_in[0], 16 * (g + 1))
                act.wait_ge(packed_ready, 4 * (g - 1) + 1)
                nc.scalar.activation(mask_ring[:, 0, :], adj_ring[:, 0, :], ACT.Relu).then_inc(relu0_ready, 1)
                act.wait_ge(relu0_ready, g)
                nc.scalar.activation(mask_ring[:, 0, :], mask_ring[:, 0, :], ACT.Sign).then_inc(mask0_ready, 1)

            def finish_group(b, g, u, first=False):
                act.wait_ge(em_ready, g + 1)
                nc.scalar.activation(q[:, :, :], em[:, :, :], ACT.Exp).then_inc(q_ready, 1)
                act.wait_ge(wts_ready, g + 1)
                stand_apart(act)
                for i in range(GT):
                    left = act.value_load(need[i:i + 1, u:u + 1], min_val=0, max_val=SLOTS * PEN)
                    base = (GT * g + i) * SLOTS

                    def diagonals(k0, k1):
                        for k in range(k0, k1):
                            if not (first and i == 0 and u == 0 and k < DIAG):
                                act.wait_ge(diag_used, base + k - DIAG + 1)
                            nc.scalar.activation(diag[:, k % DIAG, :], ident[:, :], ACT.Copy,
                                                 scale=wts[:, i, k:k + 1]).then_inc(diag_ready, 1)

                    diagonals(0, DIAG)
                    as_needed(act, left, DIAG_STEPS, diagonals, lambda slots: act.drain().then_inc(diag_ready, slots))
                act.wait_ge(agg_ready, g + 1)
                y = agg[u][:, 0:GT * D].rearrange("p (i d) -> p i d", i=GT)
                nc.scalar.activation(negy[:, :, :], y, ACT.Relu, scale=-1.0).then_inc(negy_ready, 1)
                act.wait_ge(negy_ready, g + 1)
                if not first or u:
                    act.wait_ge(out_ready, g)
                nc.scalar.activation(expy[:, :, :], negy[:, :, :], ACT.Exp, scale=-1.0).then_inc(expy_ready, 1)

            def emit(b, ahead, behind):
                for u in range(2):
                    if ahead and (behind or u):
                        make_mask0(2 * b + u)
                    if not behind:
                        continue
                    finish_group(b, 2 * b + u - 2, u, behind == "first")

            PQ = NQ // NX
            squares(0)
            relus(0, 2)
            for c in range(NX):
                if c + 1 < NX:
                    squares(c + 1)
                deviations(c)
                relus(max(2, PQ * c), PQ * (c + 1))
            emit(0, True, False)
            emit(1, True, "first")
            with act.Fori(2, NB) as b:
                emit(b, True, True)

            def f_scores(j):
                t = act.value_load(f_list[0:1, bass.ds(j, 1)], min_val=0, max_val=NT - 1)
                for c in range(FV, FQ):
                    act.wait_ge(f_in[c], 16 * (j + 1))
                    if c == FV and not isinstance(j, int):
                        act.wait_ge(f_T_ps_ready, j * F_CHUNKS)
                    stand_apart(act)
                    nc.scalar.activation(f_e[:, c, :], f_adj[:, c, :], ACT.Relu, scale=-F_BIG,
                                         bias=f_big[:, 0:1]).then_inc(f_pen_ready, 1)
                for c in range(FQ):
                    act.wait_ge(f_d_ready, j * FQ + c + 1)
                    stand_apart(act)
                    nc.scalar.activation(f_z[:, c, :], f_e[:, c, :], ACT.Identity,
                                         bias=s_all[:, bass.ds(t, 1)]).then_inc(f_z_ready, 1)
                act.wait_ge(f_m_ready, j + 1)
                for c in range(FQ):
                    act.wait_ge(f_e_ready, j * FQ + c + 1)
                    nc.scalar.activation(f_e[:, c, :], f_e[:, c, :], ACT.Exp, bias=f_row[:, 0:1],
                                         accum_out=f_sum[:, c:c + 1]).then_inc(f_q_ready, 1)

            def f_sums(j):
                def signs(c):
                    act.wait_ge(f_z_ready, j * FQ + c + 1)
                    if c:
                        act.wait_ge(f_signs_ready, j * FQ + c)
                    nc.scalar.activation(f_sign, f_z[:, c, :], ACT.Sign, bias=f_far[:, 0:1],
                                         accum_out=f_signs[:, c:c + 1]).then_inc(f_signs_ready, 1)

                for c in range(0, F_CHUNKS, 2):
                    act.wait_ge(f_T_ps_ready, j * F_CHUNKS + c + 1)
                    if c:
                        act.wait_ge(f_T_used, j * F_CHUNKS + c - 1)
                    nc.scalar.activation(f_T[:, 0, :], banks[0][:, :], ACT.Copy).then_inc(f_T_ready[0], 1)
                    if c // 2 < FQ:
                        signs(c // 2)
                act.wait_ge(f_y_ready, j + 1)
                nc.scalar.activation(negy[:, 0, :], f_y[:, :], ACT.Relu, scale=-1.0).then_inc(f_negy_ready, 1)
                act.wait_ge(f_negy_ready, j + 1)
                nc.scalar.activation(expy[:, 0, :], negy[:, 0, :], ACT.Exp, scale=-1.0).then_inc(f_expy_ready, 1)

            def f_tile(j):
                f_scores(j)
                f_sums(j)

            finish_group(NB, NG - 2, 0)
            act.wait_ge(flags_ready, 1)
            act.wait_ge(list_ready, 1)
            count = act.value_load(f_count[0:1, 0:1], min_val=0, max_val=NT)
            with act.If(count > 0):
                f_scores(0)
            finish_group(NB, NG - 1, 1)
            with act.If(count > 0):
                f_sums(0)
            for_other_flagged(act, count, f_tile)

        @block.vector
        def _(dve):
            v = Order(dve, vchain)
            def means(c):
                cs = slice(c * XT, (c + 1) * XT)
                dve.wait_ge(x_loaded[c], 16)
                v.then(nc.vector.tensor_reduce(sums[:, cs], xs[:, cs, :], AX, ALU.add))
                v.settle()
                nc.vector.tensor_scalar(neg_mean[:, cs], sums[:, cs], -1.0 / D, None, ALU.mult).then_inc(mean_ready, 1)

            def variances(c):
                dve.wait_ge(sq_ready, c + 1)
                nc.vector.tensor_reduce(sq_sums[:, c * XT:(c + 1) * XT], sq[:, :, :], AX, ALU.add).then_inc(var_ready, 1)

            def rows(c):
                cs = slice(c * XT, (c + 1) * XT)
                dve.wait_ge(std_ready, c + 1)
                nc.vector.reciprocal(rstd[:, cs], std[:, cs]).then_inc(rstd_ready, 1)
                dve.wait_ge(rstd_ready, c + 1)
                for m in range(c * XT // PT, (c + 1) * XT // PT):
                    tiles = slice(m * PT, (m + 1) * PT)
                    dve.wait_ge(h_ps_ready, m + 1)
                    nc.vector.tensor_tensor(ts[:, tiles, :], h_ps[m % HB][:, 0:PT * WIDE].rearrange("p (t r) -> p t r", r=WIDE),
                                            rstd[:, tiles].unsqueeze(2).to_broadcast([P, PT, WIDE]),
                                            ALU.mult).then_inc(h_ready, 1)
                dve.wait_ge(h_ready, (c + 1) * XT // PT)
                v.then(nc.vector.tensor_scalar(hz[:, cs], ts[:, cs, D + 2], 0.0, -BIG, ALU.is_equal, ALU.mult))
                v.then(nc.vector.tensor_copy(s_all[:, cs], ts[:, cs, D + 1]))
                v.settle()
                nc.vector.tensor_tensor(d_ok[:, cs], ts[:, cs, D], hz[:, cs], ALU.add).then_inc(d_ok_ready, 1)
                dve.wait_ge(d_ok_ready, c + 1)
                nc.vector.tensor_copy(ts[:, cs, D], d_ok[:, cs]).then_inc(rows_ready, 1)

            def make_mask(g, r):
                dve.wait_ge(adj_in[r], 16 * (g + 1))
                if not (isinstance(g, int) and g == 0):
                    dve.wait_ge(packed_ready, 4 * (g - 1) + r + 1)
                nc.vector.tensor_scalar(mask_ring[:, r, :], adj_ring[:, r, :], 0, None,
                                        ALU.is_gt).then_inc(mask_ready if r else mask0_ready, 1)

            def take_keys(g, i):
                dve.wait_ge(packed_ready, 4 * g + 2 * i + 2)
                stand_apart(dve)
                for bk in range(2):
                    segs = packed[2 * i + bk][:, :].rearrange("p (a s r) -> p s a r", s=SEGS, r=RUN)
                    for n in range(SEGS):
                        k0 = (bk * SEGS + n) * 8
                        last = nc.vector.max(V[:, i, 0, k0:k0 + 8], segs[:, n, :, :])
                last.then_inc(keys_taken, 1)

            def decode(g, u, o):
                o.settle()
                dve.wait_ge(keys_taken, GT * (g + 1))
                o.then(nc.vector.tensor_copy(kint[:, :, :], V[:, :, 0, :]))
                o.then(nc.vector.tensor_scalar(hib[:, :, 0, :], V[:, :, 0, :].bitcast(I32), EXP_MASK, None, ALU.bitwise_and))
                o.settle()
                o.then(nc.vector.tensor_scalar(cell[:, :, :], kint[:, :, :], CELLS - 1, None, ALU.bitwise_and))
                o.then(nc.vector.tensor_tensor(V[:, :, 1, :], V[:, :, 0, :], hib[:, :, 0, :].bitcast(FP32), ALU.subtract))
                o.settle()
                o.then(nc.vector.tensor_scalar(expo[:, :, :, :], V[:, :, :, :].bitcast(I32), 23, None, ALU.logical_shift_right))
                o.then(nc.vector.tensor_scalar(hib[:, :, 1, :], V[:, :, 1, :].bitcast(I32), EXP_MASK, None, ALU.bitwise_and))
                o.settle()
                for level in range(2):
                    o.then(nc.vector.scalar_tensor_tensor(cand[:, :, level, :], expo[:, :, level, :], float(CELLS),
                                                          cell[:, :, :], ALU.mult, ALU.add))
                o.then(nc.vector.tensor_tensor(rest[:, :, :], V[:, :, 1, :], hib[:, :, 1, :].bitcast(FP32), ALU.subtract))
                o.settle(apart=True)
                flat = [cand[:, i, :, :].rearrange("p l k -> p (l k)") for i in range(GT)]
                for k in range(0, SLOTS, 8):
                    for i in range(GT):
                        o.then(nc.vector.max(top[:, i, k:k + 8], flat[i]))
                    if k == 0:
                        o.then(nc.vector.tensor_reduce(mx[:, 0, :], rest[:, :, :], AX, ALU.max))
                    if k == 8:
                        o.then(nc.vector.tensor_reduce(mx[:, 1, :], V[:, :, 0, 7:KEYS:8], AX, ALU.max))
                    if k == 16:
                        o.then(nc.vector.tensor_tensor(mx[:, 2, :], mx[:, 0, :], mx[:, 1, :], ALU.max))
                    o.settle(apart=True)
                    if k + 8 < SLOTS:
                        for i in range(GT):
                            o.then(nc.vector.match_replace(out=flat[i], in_to_replace=top[:, i, k:k + 8],
                                                           in_values=flat[i], imm_value=0.0))
                        if k == 16:
                            o.then(nc.vector.tensor_scalar(mx[:, 3, :], mx[:, 2, :], float(CELLS), None, ALU.is_ge))
                        o.settle(apart=True)
                o.then(nc.vector.tensor_scalar(pen[:, u, :, :], top[:, :, :], float(EXP_OFF), float(PEN), ALU.is_lt, ALU.mult))
                o.then(nc.vector.scalar_tensor_tensor(of_group(flag_all, g), top[:, :, SLOTS - 1], float(EXP_OFF),
                                                      mx[:, 3, :], ALU.is_ge, ALU.max))
                o.settle()
                o.then(nc.vector.tensor_reduce(pen_sum[:, :], pen[:, u, :, :], AX, ALU.add))
                nc.vector.scalar_tensor_tensor(idx[:, u, :, :], top[:, :, :], float(-EXP_OFF), pen[:, u, :, :],
                                               ALU.add, ALU.add).then_inc(idx_ready, 1)
                o.settle()
                nc.vector.scalar_tensor_tensor(pens[:, :], of_group(flag_all, g), -2.0 * SLOTS * PEN,
                                               pen_sum[:, :], ALU.mult, ALU.add).then_inc(pens_ready, 1)

            def scores(b, g, u, o):
                dve.wait_ge(gathered[u], 16 * GT * SLOTS * b)
                o.then(nc.vector.scalar_tensor_tensor(xm[:, :, :], pen[:, u, :, :], -BIG / PEN, G[:, u, :, :, D],
                                                      ALU.mult, ALU.add))
                o.settle()
                o.then(nc.vector.tensor_tensor(att[:, :, :], xm[:, :, :],
                                               of_group(s_all, g).unsqueeze(2).to_broadcast([P, GT, SLOTS]),
                                               ALU.add))
                o.settle()
                o.then(nc.vector.scalar_tensor_tensor(e[:, :, :], att[:, :, :], SLOPE, att[:, :, :], ALU.mult, ALU.max))
                o.settle()
                o.then(nc.vector.tensor_reduce(r_max[:, :], e[:, :, :], AX, ALU.max))
                o.then(nc.vector.tensor_scalar(valid[:, :, :], e[:, :, :], VALID_ABOVE, None, ALU.is_gt))
                o.settle()
                nc.vector.tensor_tensor(em[:, :, :], e[:, :, :], r_max[:, :].unsqueeze(2).to_broadcast([P, GT, SLOTS]),
                                        ALU.subtract).then_inc(em_ready, 1)
                o.then(nc.vector.tensor_reduce(r_deg[:, :], valid[:, :, :], AX, ALU.add))

            def weights(g, u, o):
                dve.wait_ge(q_ready, g + 1)
                o.then(nc.vector.tensor_reduce(r_sum[:, :], q[:, :, :], AX, ALU.add))
                o.settle()
                o.then(nc.vector.reciprocal(r_inv[:, :], r_sum[:, :]))
                o.settle()
                o.then(nc.vector.tensor_tensor(att[:, :, :], q[:, :, :],
                                               r_inv[:, :].unsqueeze(2).to_broadcast([P, GT, SLOTS]), ALU.mult))
                o.then(nc.vector.scalar_tensor_tensor(r_gain[:, :], r_inv[:, :], THR, r_deg[:, :], ALU.is_gt, ALU.mult))
                o.settle()
                o.then(nc.vector.scalar_tensor_tensor(keep[:, :, :], att[:, :, :], THR, att[:, :, :], ALU.is_ge, ALU.mult))
                o.settle()
                nc.vector.tensor_tensor(wts[:, :, :], keep[:, :, :],
                                        r_gain[:, :].unsqueeze(2).to_broadcast([P, GT, SLOTS]), ALU.mult).then_inc(wts_ready, 1)

            def finish(b, g, u, o):
                dve.wait_ge(expy_ready, g + 1)
                dve.wait_ge(xh_in[u], 32 * b)
                y = agg[u][:, 0:GT * D].rearrange("p (i d) -> p i d", i=GT)
                o.then(nc.vector.scalar_tensor_tensor(elu1[:, :, :], y, 0.0, expy[:, :, :], ALU.max, ALU.add))
                o.settle()
                if not (isinstance(b, int) and b == 1):
                    dve.wait_ge(out_stored[u], 16 * (b - 1))
                nc.vector.scalar_tensor_tensor(out_sb[:, u, :, :], elu1[:, :, :], -1.0, x_in[:, u, :, :],
                                               ALU.add, ALU.add).then_inc(out_ready, 1)

            def emit(b, ahead, behind, o):
                for u in range(2):
                    g = 2 * b + u
                    masks = ahead and (behind or u)
                    if masks:
                        make_mask(g, 1)
                        make_mask(g, 2)
                    if behind:
                        scores(b, g - 2, u, o)
                        weights(g - 2, u, o)
                    if masks:
                        make_mask(g, 3)
                    if ahead:
                        take_keys(g, 0)
                        take_keys(g, 1)
                        decode(g, u, o)
                    if behind:
                        finish(b, g - 2, u, o)
                    if ahead:
                        dve.wait_ge(pensT_ready, g + 1)
                        o.then(nc.vector.tensor_reduce(least[:, 0:1], pensT, AX, ALU.min))
                        o.settle()
                        o.then(nc.vector.tensor_scalar(least[:, 1:2], least[:, 0:1], 0.0, float(SLOTS * PEN),
                                                       ALU.is_lt, ALU.mult))
                        o.settle()
                        nc.vector.tensor_tensor(need[:, u:u + 1], least[:, 0:1], least[:, 1:2],
                                                ALU.max).then_inc(need_ready, 1)
                    if not behind and u:
                        dve.wait_ge(dT_ps_ready, 1)
                        nc.vector.tensor_copy(dT[:, :], misc[0:NT, 0:P]).then_inc(dT_ready, 1)

            means(0)
            dve.wait_ge(wT_ps_ready, 1)
            nc.vector.tensor_copy(wT[:, :], misc[:, 0:P]).then_inc(wT_ready, 1)
            means(1)
            dve.wait_ge(wa_ps_ready, 1)
            nc.vector.tensor_copy(w_ext[:, D:WIDE], misc[:, P:P + 3]).then_inc(wa_ready, 1)
            means(2)
            variances(0)
            means(3)
            for c in range(NX):
                if c + 1 < NX:
                    variances(c + 1)
                if c < NX - 1:
                    rows(c)
                make_mask(0, c)
            rows(NX - 1)
            o = Order(dve, vloop)
            emit(0, True, False, o)
            first = o.n
            emit(1, True, True, o)
            peeled, per_body = o.n, o.n - first
            with dve.Fori(2, NB) as b:
                o = Order(dve, vloop, peeled + (b - 2) * per_body)
                emit(b, True, True, o)
            assert o.n == per_body

            dve.wait_ge(flagT_ready, 1)
            nc.vector.tensor_reduce(f_flag_c[:, :], small[0:NT, 384:384 + P], AX, ALU.max).then_inc(flag_col_ready, 1)
            dve.wait_ge(flag_row_ready, 1)
            flag_row = small[0:1, 0:NT]
            v.then(nc.vector.tensor_tensor(f_keys[:, :], flag_row, f_order[:, :], ALU.mult))
            v.then(nc.vector.tensor_reduce(f_counted[:, :], flag_row, AX, ALU.add))
            v.settle()

            def list_tiles(k):
                ks = slice(k, k + 8)
                v.then(nc.vector.max(f_sorted[:, ks], f_keys[:, :]))
                v.settle()
                v.then(nc.vector.match_replace(out=f_keys[:, :], in_to_replace=f_sorted[:, ks],
                                               in_values=f_keys[:, :], imm_value=0.0))
                nc.vector.tensor_scalar(f_list[:, ks], f_sorted[:, ks], -1.0, float(NT), ALU.mult,
                                        ALU.add).then_inc(list_ready, 1)
                v.settle()

            list_tiles(0)
            nc.vector.tensor_copy(f_count[:, :], f_counted[:, :]).then_inc(flags_ready, 1)

            neg_m, z_max, m_slope, m_one, signs, deg, z_sum, inv, gain, bar, scale = (
                f_row[:, c:c + 1] for c in range(11))

            def f_scores(j):
                t = dve.value_load(f_list[0:1, bass.ds(j, 1)], min_val=0, max_val=NT - 1)
                o = Order(dve, fchain, j * F_CHAIN)
                for c in range(FQ):
                    if c < FV:
                        dve.wait_ge(f_in[c], 16 * (j + 1))
                        if c == 0 and not isinstance(j, int):
                            dve.wait_ge(f_T_ps_ready, j * F_CHUNKS)
                        o.then(nc.vector.tensor_scalar(f_e[:, c, :], f_adj[:, c, :], 0, F_BIG, ALU.is_le, ALU.mult))
                        o.settle(apart=True)
                    else:
                        dve.wait_ge(f_pen_ready, j * (FQ - FV) + c - FV + 1)
                        stand_apart(dve)
                    nc.vector.tensor_tensor_reduce(out=f_e[:, c, :], in0=f_d[:, c, :], in1=f_e[:, c, :], scale=1.0,
                                                   scalar=-3e38, op0=ALU.subtract, op1=ALU.max,
                                                   accum_out=f_max[:, c:c + 1]).then_inc(f_d_ready, 1)
                dve.wait_ge(f_d_ready, (j + 1) * FQ)
                o.then(nc.vector.tensor_reduce(z_max, f_max[:, :], AX, ALU.max))
                o.settle()
                o.then(nc.vector.tensor_scalar(m_slope, z_max, s_all[:, bass.ds(t, 1)], -SLOPE, ALU.add, ALU.mult))
                o.then(nc.vector.tensor_scalar(m_one, z_max, s_all[:, bass.ds(t, 1)], -1.0, ALU.add, ALU.mult))
                o.settle()
                nc.vector.tensor_tensor(neg_m, m_slope, m_one, ALU.min).then_inc(f_m_ready, 1)
                for c in range(FQ):
                    dve.wait_ge(f_z_ready, j * FQ + c + 1)
                    nc.vector.scalar_tensor_tensor(f_e[:, c, :], f_z[:, c, :], SLOPE, f_z[:, c, :],
                                                   ALU.mult, ALU.max).then_inc(f_e_ready, 1)
                return o

            def f_weights(j, o):
                dve.wait_ge(f_q_ready, (j + 1) * FQ)
                o.then(nc.vector.tensor_reduce(z_sum, f_sum[:, :], AX, ALU.add))
                o.settle()
                nc.vector.tensor_scalar(bar, z_sum, THR, None, ALU.mult).then_inc(f_least_ready, 1)
                dve.wait_ge(f_least_ready, j + 1)
                for c in range(FQ):
                    nc.vector.scalar_tensor_tensor(f_e[:, c, :], f_e[:, c, :], bar, f_e[:, c, :],
                                                   ALU.is_ge, ALU.mult).then_inc(f_w_ready, 1)

            def f_finish(j, o):
                t = dve.value_load(f_list[0:1, bass.ds(j, 1)], min_val=0, max_val=NT - 1)
                for c in range(1, F_CHUNKS, 2):
                    dve.wait_ge(f_T_ps_ready, j * F_CHUNKS + c + 1)
                    if c >= 2:
                        dve.wait_ge(f_T_used, j * F_CHUNKS + c - 1)
                    nc.vector.tensor_copy(f_T[:, 1, :], banks[1][:, :]).then_inc(f_T_ready[1], 1)
                dve.wait_ge(f_signs_ready, (j + 1) * FQ)
                o.then(nc.vector.tensor_reduce(signs, f_signs[:, :], AX, ALU.add))
                o.then(nc.vector.reciprocal(inv, z_sum))
                o.settle()
                o.then(nc.vector.tensor_scalar(deg, signs, float(N), 0.5, ALU.add, ALU.mult))
                o.settle()
                o.then(nc.vector.scalar_tensor_tensor(gain, inv, THR, deg, ALU.is_gt, ALU.mult))
                o.settle()
                nc.vector.tensor_tensor(scale, gain, inv, ALU.mult).then_inc(f_scale_ready, 1)
                assert o.n == F_CHAIN, o.n
                dve.wait_ge(f_scale_ready, j + 1)
                dve.wait_ge(f_T_used, (j + 1) * F_CHUNKS)
                nc.vector.scalar_tensor_tensor(f_y[:, :], agg[0][:, 0:D], scale,
                                               f_h[:, bass.ds(t, 1), 0:D].rearrange("p t d -> p (t d)"),
                                               ALU.mult, ALU.add).then_inc(f_y_ready, 1)
                dve.wait_ge(f_expy_ready, j + 1)
                dve.wait_ge(f_x_in, 16 * (j + 1))
                nc.vector.scalar_tensor_tensor(elu1[:, 0, :], f_y[:, :], 0.0, expy[:, 0, :],
                                               ALU.max, ALU.add).then_inc(f_out_ready, 1)
                dve.wait_ge(f_out_ready, 2 * j + 1)
                nc.vector.scalar_tensor_tensor(f_out[:, :], elu1[:, 0, :], -1.0, f_x[:, :],
                                               ALU.add, ALU.add).then_inc(f_out_ready, 1)
                dve.wait_ge(f_stored, 16 * (j + 1))
                stand_apart(dve)

            def f_tile(j):
                o = f_scores(j)
                f_weights(j, o)
                f_finish(j, o)

            o = Order(dve, vloop, peeled + (NB - 2) * per_body)
            dve.wait_ge(flags_ready, 1)
            dve.wait_ge(list_ready, 1)
            count = dve.value_load(f_count[0:1, 0:1], min_val=0, max_val=NT)
            scores(NB, NG - 2, 0, o)
            weights(NG - 2, 0, o)
            with dve.If(count > 0):
                dve.wait_ge(f_d_in, 16)
                fo = f_scores(0)
            finish(NB, NG - 2, 0, o)
            scores(NB, NG - 1, 1, o)
            weights(NG - 1, 1, o)
            with dve.If(count > 0):
                f_weights(0, fo)
            finish(NB, NG - 1, 1, o)
            with dve.If(count > 0):
                dve.wait_ge(f_h_in, 16)
                f_finish(0, fo)
            with dve.If(count > 1):
                for k in range(8, NT, 8):
                    list_tiles(k)
            for_other_flagged(dve, count, f_tile)

        @block.tensor
        def _(pe):
            pe.wait_ge(consts, CONSTS)
            pe.wait_ge(w_in, 48)
            nc.tensor.transpose(misc[:, 0:P], w_ext[:, 0:D], ident[:, :]).then_inc(wT_ps_ready, 1)
            pe.wait_ge(wT_ready, 1)
            nc.tensor.matmul(misc[:, P:P + 3], wT[:, :], a_sb[:, :], start=True, stop=True).then_inc(wa_ps_ready, 1)
            pe.wait_ge(wa_ready, 1)

            def transposes(n):
                pe.wait_ge(xc_ready, (n * QT) // XT + 1)
                if n >= 2:
                    pe.wait_ge(relT_ready, n - 1)
                for i in range(QT):
                    last = nc.tensor.transpose(xT_ps[n % 2][:, i * P:(i + 1) * P], xs[:, QT * n + i, :], ident[:, :])
                last.then_inc(xT_ps_ready, 1)

            def pack(g, r, more):
                i, half = divmod(r, 2)
                wait_mask(pe, g, r)
                if half == 0 and more:
                    pe.wait_ge(keys_taken, GT * (g - 1) + i + 1)
                for bk in range(2):
                    bank = packed[2 * i + bk][:, :].rearrange("p (a c) -> p a c", a=2)

                    def of_bank(cells):
                        return cells.rearrange("p (a b c) -> p b a c", b=2, c=SPLIT)[:, bk, :, :]

                    if half == 0:
                        nc.tensor.matmul(bank, cell_w[0:2, :], of_bank(cell_no[0:2, :]), start=True, stop=False)
                    for k in range(PACK // 2):
                        last = nc.tensor.matmul(bank, pack_w[:, half * (PACK // 2) + k, :],
                                                of_bank(mask_ring[:, r, k * CELLS:(k + 1) * CELLS]), start=False,
                                                stop=(half == 1 and k == PACK // 2 - 1))
                last.then_inc(packed_ready, 1)

            transposes(0)
            for n in range(NQ):
                if n + 1 < NQ:
                    transposes(n + 1)
                pe.wait_ge(relT_ready, n + 1)
                for m in range(n * QT // PT, (n + 1) * QT // PT):
                    if m >= HB:
                        pe.wait_ge(h_ready, m - HB + 1)
                    for k in range(PT):
                        i = (m * PT + k) % QT
                        last = nc.tensor.matmul(h_ps[m % HB][:, k * WIDE:(k + 1) * WIDE],
                                                relT[:, n % 2, i * P:(i + 1) * P], w_ext[:, :], start=True, stop=True)
                    last.then_inc(h_ps_ready, 1)
            pe.wait_ge(h_ready, NT // PT)

            def weigh(b, g, u, first):
                for i in range(GT):
                    acc = agg[u][:, i * D:(i + 1) * D]
                    left = pe.value_load(need[i:i + 1, u:u + 1], min_val=0, max_val=SLOTS * PEN)
                    base = (GT * g + i) * SLOTS
                    if i == 0:
                        pe.wait_ge(xh_in[u], 32 * b)
                        if not first:
                            pe.wait_ge(out_ready, g - 1)
                        pe.wait_ge(gathered[u], 16 * GT * SLOTS * b)

                    def rows(k0, k1):
                        for k in range(k0, k1):
                            pe.wait_ge(diag_ready, base + k + 1)
                            nc.tensor.matmul(acc, diag[:, k % DIAG, :], G[:, u, i, k, 0:D], start=(k == 0),
                                             stop=False).then_inc(diag_used, 1)

                    rows(0, DIAG)
                    as_needed(pe, left, DIAG_STEPS, rows, lambda slots: pe.drain().then_inc(diag_used, slots))
                    last = nc.tensor.matmul(acc, ident[:, :], h_in[:, u, i, 0:D], start=False, stop=True)
                last.then_inc(agg_ready, 1)

            def emit(b, ahead, behind, first=False):
                for u in range(2):
                    g = 2 * b + u
                    if ahead:
                        for r in range(4):
                            pack(g, r, behind or u)
                    if behind:
                        weigh(b, g - 2, u, first)
                    if ahead:
                        pe.wait_ge(pens_ready, g + 1)
                        if behind or u:
                            pe.wait_ge(need_ready, g)
                        nc.tensor.transpose(pensT, pens[:, :], ident[:, :]).then_inc(pensT_ready, 1)
                    if not behind and u:
                        pe.wait_ge(d_ok_ready, NX)
                        nc.tensor.transpose(misc[0:NT, 0:P], d_ok[:, :], ident[:, :]).then_inc(dT_ps_ready, 1)

            emit(0, True, False)
            emit(1, True, True, True)
            with pe.Fori(2, NB) as b:
                emit(b, True, True)
            pe.wait_ge(need_ready, NG)
            nc.tensor.transpose(small[0:NT, 384:384 + P], flag_all[:, :], ident[:, :]).then_inc(flagT_ready, 1)
            pe.wait_ge(flag_col_ready, 1)
            nc.tensor.transpose(small[0:1, 0:NT], f_flag_c[:, :], ident[0:NT, 0:NT]).then_inc(flag_row_ready, 1)
            emit(NB, False, True)

            pe.wait_ge(flags_ready, 1)
            pe.wait_ge(f_h_in, 16)
            pe.wait_ge(out_ready, NG - 1)

            def f_tile(j):
                def f_transposes(c):
                    if c >= 2:
                        pe.wait_ge(f_T_ready[c % 2], j * (F_CHUNKS // 2) + c // 2)
                    pe.wait_ge(f_w_ready, j * FQ + c // 4 + 1)
                    for i in range(QT):
                        c0 = (c % 4 * QT + i) * P
                        last = nc.tensor.transpose(banks[c % 2][:, i * P:(i + 1) * P],
                                                   f_e[:, c // 4, c0:c0 + P], ident[:, :])
                    last.then_inc(f_T_ps_ready, 1)

                f_transposes(0)
                for c in range(F_CHUNKS):
                    if c + 1 < F_CHUNKS:
                        f_transposes(c + 1)
                    pe.wait_ge(f_T_ready[c % 2], j * (F_CHUNKS // 2) + c // 2 + 1)
                    for i in range(QT):
                        last = nc.tensor.matmul(agg[0][:, 0:D], f_T[:, c % 2, i * P:(i + 1) * P],
                                                f_h[:, QT * c + i, 0:D], start=(c == 0 and i == 0),
                                                stop=(c == F_CHUNKS - 1 and i == QT - 1))
                    last.then_inc(f_T_used, 1)
                pe.wait_ge(f_y_ready, j + 1)
                stand_apart(pe)

            count = pe.value_load(f_count[0:1, 0:1], min_val=0, max_val=NT)
            with pe.If(count > 0):
                f_tile(0)
            for_other_flagged(pe, count, f_tile)


_INS = ["x", "adj", "L0_gnn_W", "L0_gnn_a"]
_OUTS = [((8192, 128), "float32")]


def kernel(**inputs):
    import numpy as _np
    import concourse.bacc as _bacc
    from concourse import mybir as _mybir
    from concourse.bass_utils import run_bass_kernel_spmd as _run

    nc = _bacc.Bacc("TRN2", target_bir_lowering=False, num_devices=1)
    arrays, args = {}, []
    for name in _INS:
        a = _np.ascontiguousarray(inputs[name])
        arrays[f"in_{name}_dram"] = a
        args.append(nc.dram_tensor(f"in_{name}_dram", a.shape, _mybir.dt.from_np(a.dtype), kind="ExternalInput").ap())
    for i, (shape, dtype) in enumerate(_OUTS):
        dt = _mybir.dt.from_np(_np.dtype(dtype))
        args.append(nc.dram_tensor(f"out_{i}_dram", shape, dt, kind="ExternalOutput").ap())
    gat_kernel(nc, *args)
    r = _run(nc, [arrays], core_ids=[0])
    return r.results[0]["out_0_dram"]
```
